# Optimizing a Trainium2 kernel written in Bass

```python
import numpy as np
import jax
import jax.numpy as jnp

def _softmax(x, axis=-1):
    return jax.nn.softmax(x, axis=axis)

def _gelu(x):
    return jax.nn.gelu(x, approximate=True)

def _silu(x):
    return jax.nn.silu(x)

def _sigmoid(x):
    return jax.nn.sigmoid(x)

def _layernorm(x, axis=-1, eps=1e-05):
    m = jnp.mean(x, axis=axis, keepdims=True)
    v = jnp.var(x, axis=axis, keepdims=True)
    return (x - m) / jnp.sqrt(v + eps)

def _scatter_add(tgt, idx, src, axis=0):
    return tgt.at[idx].add(src)

def _segment_sum(src, seg, n):
    return jax.ops.segment_sum(src, seg, n)
kernel_name = 'mk_prb_d2_jaxref_r8_3a0878'

def setup_inputs(seed: int=0):
    np.random.seed(seed)
    _w = jnp.asarray

    def _L0_attn_setup():
        import jax, jax.numpy as jnp
        import numpy as np
        from jax import lax
        B, T, D, H = (2, 512, 128, 16)
        DK = DV = D // H
        KS = 4
        ALPHA_MIN, BETA_MAX, EPS = (0.1, 1.0, 1e-06)

        def _causal_dwconv(x, w, b):
            C, K = w.shape
            xp = jnp.pad(x, ((0, 0), (K - 1, 0), (0, 0))).transpose(0, 2, 1)
            out = lax.conv_general_dilated(xp, w[:, None, :], (1,), 'VALID', feature_group_count=C, dimension_numbers=('NCH', 'OIH', 'NCH'))
            out = out + b[None, :, None]
            return jax.nn.silu(out).transpose(0, 2, 1)

        def _l2n(t):
            return t / jnp.maximum(jnp.linalg.norm(t, axis=-1, keepdims=True), 1e-06)
        key = jax.random.key(seed)
        ks = jax.random.split(key, 20)

        def w(i, shape, sc=0.02):
            return jax.random.normal(ks[i], shape, jnp.float32) * sc
        return {'x': jax.random.normal(ks[0], (B, T, D), jnp.float32), 'Wq': w(1, (D, H * DK)), 'Wk': w(2, (D, H * DK)), 'Wv': w(3, (D, H * DV)), 'Wo': w(4, (H * DV, D)), 'Wa': w(5, (D, H)), 'ba': jnp.full((H,), 2.0, jnp.float32), 'Wb': w(6, (D, H)), 'bb': jnp.zeros((H,), jnp.float32), 'Wgd': w(7, (D, H * DV // 2)), 'Wgu': w(8, (H * DV // 2, H * DV)), 'rms_w': jnp.ones((H, DV), jnp.float32), 'qcw': w(9, (H * DK, KS), 0.1), 'qcb': jnp.zeros((H * DK,), jnp.float32), 'kcw': w(10, (H * DK, KS), 0.1), 'kcb': jnp.zeros((H * DK,), jnp.float32), 'vcw': w(11, (H * DV, KS), 0.1), 'vcb': jnp.zeros((H * DV,), jnp.float32)}
    _L0_attn_in = _L0_attn_setup()

    def _L0_ffn_setup():
        import jax, jax.numpy as jnp
        import numpy as np
        B, T, D, H, E = (4, 256, 128, 256, 8)
        TOP_K = int(E * 0.25)
        key = jax.random.key(seed)
        ks = jax.random.split(key, 6)
        x = jax.random.normal(ks[0], (B, T, D), dtype=jnp.float32)
        gate = jax.random.normal(ks[1], (D, E), dtype=jnp.float32)
        W1 = jax.random.normal(ks[2], (E, D, H), dtype=jnp.float32) * D ** (-0.5)
        b1 = jnp.zeros((E, H), dtype=jnp.float32)
        W2 = jax.random.normal(ks[3], (E, H, D), dtype=jnp.float32) * H ** (-0.5)
        b2 = jnp.zeros((E, D), dtype=jnp.float32)
        return {'x': x, 'gate': gate, 'W1': W1, 'b1': b1, 'W2': W2, 'b2': b2}
    _L0_ffn_in = _L0_ffn_setup()

    def _L1_attn_setup():
        import jax, jax.numpy as jnp
        import numpy as np
        import math
        N_EMBD = 128
        N_HEAD = 16
        HEAD = N_EMBD // N_HEAD
        LAYER_IDX = 2
        LAMBDA_INIT = 0.8 - 0.6 * math.exp(-0.3 * (LAYER_IDX - 1))
        BN_EPS = 1e-05
        RMS_EPS = 1e-05

        def _heads(y, B, T, d):
            return y.reshape(B, T, N_HEAD, d).transpose(0, 2, 1, 3)
        key = jax.random.key(seed)
        ks = jax.random.split(key, 16)
        B, T = (4, 128)
        s = 1.0 / math.sqrt(N_EMBD)
        return {'x': jax.random.normal(ks[0], (B, T, N_EMBD), jnp.float32), 'q1_w': jax.random.normal(ks[1], (N_EMBD, N_EMBD), jnp.float32) * s, 'q2_w': jax.random.normal(ks[2], (N_EMBD, N_EMBD), jnp.float32) * s, 'k1_w': jax.random.normal(ks[3], (N_EMBD, N_EMBD), jnp.float32) * s, 'k2_w': jax.random.normal(ks[4], (N_EMBD, N_EMBD), jnp.float32) * s, 'v_w': jax.random.normal(ks[5], (2 * N_EMBD, N_EMBD), jnp.float32) * s, 'c_w': jax.random.normal(ks[6], (N_EMBD, 2 * N_EMBD), jnp.float32) * s, 'subln_w': jnp.ones((2 * HEAD,), jnp.float32), 'lq1': jax.random.normal(ks[7], (HEAD,), jnp.float32) * 0.1, 'lk1': jax.random.normal(ks[8], (HEAD,), jnp.float32) * 0.1, 'lq2': jax.random.normal(ks[9], (HEAD,), jnp.float32) * 0.1, 'lk2': jax.random.normal(ks[10], (HEAD,), jnp.float32) * 0.1, 'bn_gamma': jnp.ones((N_EMBD,), jnp.float32), 'bn_beta': jnp.zeros((N_EMBD,), jnp.float32)}
    _L1_attn_in = _L1_attn_setup()

    def _L1_ffn_setup():
        import jax, jax.numpy as jnp
        import numpy as np
        B, N, D, H, E = (4, 128, 128, 16, 8)
        DK = D // H
        HID = 4 * D
        EPS = 1e-05

        def _layernorm(x, w, b):
            m = jnp.mean(x, axis=-1, keepdims=True)
            v = jnp.mean(jnp.square(x - m), axis=-1, keepdims=True)
            return (x - m) * jax.lax.rsqrt(v + EPS) * w + b

        def _msa(x, w_qkv, w_proj):
            b, n, d = x.shape
            qkv = (x @ w_qkv).reshape(b, n, 3, H, DK)
            q = qkv[:, :, 0].transpose(0, 2, 1, 3)
            k = qkv[:, :, 1].transpose(0, 2, 1, 3)
            v = qkv[:, :, 2].transpose(0, 2, 1, 3)
            attn = jnp.einsum('bhnd,bhmd->bhnm', q, k) * (1.0 / np.sqrt(DK))
            attn = jax.nn.softmax(attn, axis=-1)
            y = jnp.einsum('bhnm,bhmd->bhnd', attn, v)
            y = y.transpose(0, 2, 1, 3).reshape(b, n, d)
            return y @ w_proj

        def _moe_mlp(x, gate_w, gate_b, w1, w2):
            b, n, d = x.shape
            xf = x.reshape(b * n, d)
            logits = xf @ gate_w + gate_b
            one_hot = jax.nn.one_hot(jnp.argmax(logits, axis=-1), E, dtype=xf.dtype)
            h = jax.nn.gelu(jnp.einsum('td,edh->teh', xf, w1), approximate=True)
            y = jnp.einsum('teh,ehd->ted', h, w2)
            out = jnp.einsum('te,ted->td', one_hot, y)
            return out.reshape(b, n, d)
        key = jax.random.key(seed)
        ks = jax.random.split(key, 8)
        s = 0.02
        return {'x': jax.random.normal(ks[0], (B, N, D), jnp.float32), 'ln1_w': jnp.ones((D,), jnp.float32), 'ln1_b': jnp.zeros((D,), jnp.float32), 'w_qkv': jax.random.normal(ks[1], (D, 3 * D), jnp.float32) * s, 'w_proj': jax.random.normal(ks[2], (D, D), jnp.float32) * s, 'ln2_w': jnp.ones((D,), jnp.float32), 'ln2_b': jnp.zeros((D,), jnp.float32), 'gate_w': jax.random.normal(ks[3], (D, E), jnp.float32) * s, 'gate_b': jnp.zeros((E,), jnp.float32), 'w1': jax.random.normal(ks[4], (E, D, HID), jnp.float32) * s, 'w2': jax.random.normal(ks[5], (E, HID, D), jnp.float32) * s}
    _L1_ffn_in = _L1_ffn_setup()
    _d = {'L0_attn_x': _L0_attn_in['x'], 'L0_attn_Wq': _L0_attn_in['Wq'], 'L0_attn_Wk': _L0_attn_in['Wk'], 'L0_attn_Wv': _L0_attn_in['Wv'], 'L0_attn_Wo': _L0_attn_in['Wo'], 'L0_attn_Wa': _L0_attn_in['Wa'], 'L0_attn_ba': _L0_attn_in['ba'], 'L0_attn_Wb': _L0_attn_in['Wb'], 'L0_attn_bb': _L0_attn_in['bb'], 'L0_attn_Wgd': _L0_attn_in['Wgd'], 'L0_attn_Wgu': _L0_attn_in['Wgu'], 'L0_attn_rms_w': _L0_attn_in['rms_w'], 'L0_attn_qcw': _L0_attn_in['qcw'], 'L0_attn_qcb': _L0_attn_in['qcb'], 'L0_attn_kcw': _L0_attn_in['kcw'], 'L0_attn_kcb': _L0_attn_in['kcb'], 'L0_attn_vcw': _L0_attn_in['vcw'], 'L0_attn_vcb': _L0_attn_in['vcb'], 'L0_ffn_gate': _L0_ffn_in['gate'], 'L0_ffn_W1': _L0_ffn_in['W1'], 'L0_ffn_b1': _L0_ffn_in['b1'], 'L0_ffn_W2': _L0_ffn_in['W2'], 'L0_ffn_b2': _L0_ffn_in['b2'], 'L1_attn_q1_w': _L1_attn_in['q1_w'], 'L1_attn_q2_w': _L1_attn_in['q2_w'], 'L1_attn_k1_w': _L1_attn_in['k1_w'], 'L1_attn_k2_w': _L1_attn_in['k2_w'], 'L1_attn_v_w': _L1_attn_in['v_w'], 'L1_attn_c_w': _L1_attn_in['c_w'], 'L1_attn_subln_w': _L1_attn_in['subln_w'], 'L1_attn_lq1': _L1_attn_in['lq1'], 'L1_attn_lk1': _L1_attn_in['lk1'], 'L1_attn_lq2': _L1_attn_in['lq2'], 'L1_attn_lk2': _L1_attn_in['lk2'], 'L1_attn_bn_gamma': _L1_attn_in['bn_gamma'], 'L1_attn_bn_beta': _L1_attn_in['bn_beta'], 'L1_ffn_ln1_w': _L1_ffn_in['ln1_w'], 'L1_ffn_ln1_b': _L1_ffn_in['ln1_b'], 'L1_ffn_w_qkv': _L1_ffn_in['w_qkv'], 'L1_ffn_w_proj': _L1_ffn_in['w_proj'], 'L1_ffn_ln2_w': _L1_ffn_in['ln2_w'], 'L1_ffn_ln2_b': _L1_ffn_in['ln2_b'], 'L1_ffn_gate_w': _L1_ffn_in['gate_w'], 'L1_ffn_gate_b': _L1_ffn_in['gate_b'], 'L1_ffn_w1': _L1_ffn_in['w1'], 'L1_ffn_w2': _L1_ffn_in['w2']}
    _x0 = _d['L0_attn_x']
    _d['L0_attn_x'] = jax.random.normal(jax.random.fold_in(jax.random.key(seed), 1), (8, 256, 128), dtype=_x0.dtype)
    del _x0
    return _d

def reference(L0_attn_x, L0_attn_Wq, L0_attn_Wk, L0_attn_Wv, L0_attn_Wo, L0_attn_Wa, L0_attn_ba, L0_attn_Wb, L0_attn_bb, L0_attn_Wgd, L0_attn_Wgu, L0_attn_rms_w, L0_attn_qcw, L0_attn_qcb, L0_attn_kcw, L0_attn_kcb, L0_attn_vcw, L0_attn_vcb, L0_ffn_gate, L0_ffn_W1, L0_ffn_b1, L0_ffn_W2, L0_ffn_b2, L1_attn_q1_w, L1_attn_q2_w, L1_attn_k1_w, L1_attn_k2_w, L1_attn_v_w, L1_attn_c_w, L1_attn_subln_w, L1_attn_lq1, L1_attn_lk1, L1_attn_lq2, L1_attn_lk2, L1_attn_bn_gamma, L1_attn_bn_beta, L1_ffn_ln1_w, L1_ffn_ln1_b, L1_ffn_w_qkv, L1_ffn_w_proj, L1_ffn_ln2_w, L1_ffn_ln2_b, L1_ffn_gate_w, L1_ffn_gate_b, L1_ffn_w1, L1_ffn_w2):

    def _L0_attn_ref(x, Wq, Wk, Wv, Wo, Wa, ba, Wb, bb, Wgd, Wgu, rms_w, qcw, qcb, kcw, kcb, vcw, vcb):
        import jax, jax.numpy as jnp
        import numpy as np
        from jax import lax
        B, T, D, H = (2, 512, 128, 16)
        DK = DV = D // H
        KS = 4
        ALPHA_MIN, BETA_MAX, EPS = (0.1, 1.0, 1e-06)

        def _causal_dwconv(x, w, b):
            C, K = w.shape
            xp = jnp.pad(x, ((0, 0), (K - 1, 0), (0, 0))).transpose(0, 2, 1)
            out = lax.conv_general_dilated(xp, w[:, None, :], (1,), 'VALID', feature_group_count=C, dimension_numbers=('NCH', 'OIH', 'NCH'))
            out = out + b[None, :, None]
            return jax.nn.silu(out).transpose(0, 2, 1)

        def _l2n(t):
            return t / jnp.maximum(jnp.linalg.norm(t, axis=-1, keepdims=True), 1e-06)
        Bx, Tx, _ = x.shape
        BH = Bx * H
        q = _causal_dwconv(x @ Wq, qcw, qcb)
        k = _causal_dwconv(x @ Wk, kcw, kcb)
        v = _causal_dwconv(x @ Wv, vcw, vcb)

        def heads(t, d):
            return t.reshape(Bx, Tx, H, d).transpose(0, 2, 1, 3).reshape(BH, Tx, d)
        Q = _l2n(heads(q, DK))
        Kh = _l2n(heads(k, DK))
        V = heads(v, DV)
        alpha = jnp.clip(jax.nn.sigmoid(x @ Wa + ba), ALPHA_MIN, 1.0)
        beta = jnp.minimum(jax.nn.sigmoid(x @ Wb + bb), BETA_MAX)
        alpha = alpha.transpose(0, 2, 1).reshape(BH, Tx)
        beta = beta.transpose(0, 2, 1).reshape(BH, Tx)

        def step(S, inp):
            qt, kt, vt, at, bt = inp
            v_hat = jnp.einsum('bij,bi->bj', S, kt)
            err = vt - v_hat
            S = at[:, None, None] * S + bt[:, None, None] * (kt[:, :, None] * err[:, None, :])
            o = jnp.einsum('bij,bi->bj', S, qt)
            return (S, o)
        S0 = jnp.zeros((BH, DK, DV), x.dtype)
        _, O = lax.scan(step, S0, (Q.swapaxes(0, 1), Kh.swapaxes(0, 1), V.swapaxes(0, 1), alpha.T, beta.T))
        O = O.transpose(1, 0, 2).reshape(Bx, H, Tx, DV)
        O = O * lax.rsqrt(jnp.mean(O * O, -1, keepdims=True) + EPS) * rms_w[None, :, None, :]
        g = jax.nn.sigmoid(jax.nn.silu(x @ Wgd) @ Wgu).reshape(Bx, Tx, H, DV).transpose(0, 2, 1, 3)
        O = (O * g).transpose(0, 2, 1, 3).reshape(Bx, Tx, H * DV)
        return O @ Wo

    def _L0_ffn_ref(x, gate, W1, b1, W2, b2):
        import jax, jax.numpy as jnp
        import numpy as np
        B, T, D, H, E = (4, 256, 128, 256, 8)
        TOP_K = int(E * 0.25)
        raw_gate = jax.nn.softmax(jnp.einsum('btd,de->bte', x, gate), axis=-1)
        topk_scores, topk_idx = jax.lax.top_k(raw_gate, TOP_K)
        mask = jax.nn.one_hot(topk_idx, E, dtype=raw_gate.dtype).sum(axis=-2)
        gate_topk = mask * raw_gate
        gate_topk = gate_topk / jnp.maximum(gate_topk.sum(axis=-1, keepdims=True), 1e-12)
        h = jax.nn.relu(jnp.einsum('btd,edh->beth', x, W1) + b1[None, :, None, :])
        expert_out = jnp.einsum('beth,ehd->betd', h, W2) + b2[None, :, None, :]
        out = jnp.einsum('bte,betd->btd', gate_topk, expert_out)
        return out

    def _L1_attn_ref(x, q1_w, q2_w, k1_w, k2_w, v_w, c_w, subln_w, lq1, lk1, lq2, lk2, bn_gamma, bn_beta):
        import jax, jax.numpy as jnp
        import numpy as np
        import math
        N_EMBD = 128
        N_HEAD = 16
        HEAD = N_EMBD // N_HEAD
        LAYER_IDX = 2
        LAMBDA_INIT = 0.8 - 0.6 * math.exp(-0.3 * (LAYER_IDX - 1))
        BN_EPS = 1e-05
        RMS_EPS = 1e-05

        def _heads(y, B, T, d):
            return y.reshape(B, T, N_HEAD, d).transpose(0, 2, 1, 3)
        B, T, C = x.shape
        mean = jnp.mean(x, axis=(0, 1))
        var = jnp.var(x, axis=(0, 1))
        xn = (x - mean) * jax.lax.rsqrt(var + BN_EPS) * bn_gamma + bn_beta
        q1 = _heads(xn @ q1_w.T, B, T, HEAD)
        q2 = _heads(xn @ q2_w.T, B, T, HEAD)
        k1 = _heads(xn @ k1_w.T, B, T, HEAD)
        k2 = _heads(xn @ k2_w.T, B, T, HEAD)
        v = _heads(xn @ v_w.T, B, T, 2 * HEAD)
        scale = 1.0 / math.sqrt(HEAD)
        att1 = jax.nn.softmax(jnp.einsum('bhtd,bhsd->bhts', q1, k1) * scale, axis=-1)
        att2 = jax.nn.softmax(jnp.einsum('bhtd,bhsd->bhts', q2, k2) * scale, axis=-1)
        lam = jnp.exp(jnp.sum(lq1 * lk1)) - jnp.exp(jnp.sum(lq2 * lk2)) + LAMBDA_INIT
        att = att1 - lam * att2
        y = jnp.einsum('bhts,bhse->bhte', att, v)
        y = y * jax.lax.rsqrt(jnp.mean(y * y, axis=-1, keepdims=True) + RMS_EPS) * subln_w
        y = y * (1.0 - LAMBDA_INIT)
        y = y.transpose(0, 2, 1, 3).reshape(B, T, 2 * C)
        return y @ c_w.T

    def _L1_ffn_ref(x, ln1_w, ln1_b, w_qkv, w_proj, ln2_w, ln2_b, gate_w, gate_b, w1, w2):
        import jax, jax.numpy as jnp
        import numpy as np
        B, N, D, H, E = (4, 128, 128, 16, 8)
        DK = D // H
        HID = 4 * D
        EPS = 1e-05

        def _layernorm(x, w, b):
            m = jnp.mean(x, axis=-1, keepdims=True)
            v = jnp.mean(jnp.square(x - m), axis=-1, keepdims=True)
            return (x - m) * jax.lax.rsqrt(v + EPS) * w + b

        def _msa(x, w_qkv, w_proj):
            b, n, d = x.shape
            qkv = (x @ w_qkv).reshape(b, n, 3, H, DK)
            q = qkv[:, :, 0].transpose(0, 2, 1, 3)
            k = qkv[:, :, 1].transpose(0, 2, 1, 3)
            v = qkv[:, :, 2].transpose(0, 2, 1, 3)
            attn = jnp.einsum('bhnd,bhmd->bhnm', q, k) * (1.0 / np.sqrt(DK))
            attn = jax.nn.softmax(attn, axis=-1)
            y = jnp.einsum('bhnm,bhmd->bhnd', attn, v)
            y = y.transpose(0, 2, 1, 3).reshape(b, n, d)
            return y @ w_proj

        def _moe_mlp(x, gate_w, gate_b, w1, w2):
            b, n, d = x.shape
            xf = x.reshape(b * n, d)
            logits = xf @ gate_w + gate_b
            one_hot = jax.nn.one_hot(jnp.argmax(logits, axis=-1), E, dtype=xf.dtype)
            h = jax.nn.gelu(jnp.einsum('td,edh->teh', xf, w1), approximate=True)
            y = jnp.einsum('teh,ehd->ted', h, w2)
            out = jnp.einsum('te,ted->td', one_hot, y)
            return out.reshape(b, n, d)
        x = x + _msa(_layernorm(x, ln1_w, ln1_b), w_qkv, w_proj)
        x = x + _moe_mlp(_layernorm(x, ln2_w, ln2_b), gate_w, gate_b, w1, w2)
        return x
    x = L0_attn_x
    xn = _layernorm(x, axis=-1)
    x = x + _L0_attn_ref(xn, L0_attn_Wq, L0_attn_Wk, L0_attn_Wv, L0_attn_Wo, L0_attn_Wa, L0_attn_ba, L0_attn_Wb, L0_attn_bb, L0_attn_Wgd, L0_attn_Wgu, L0_attn_rms_w, L0_attn_qcw, L0_attn_qcb, L0_attn_kcw, L0_attn_kcb, L0_attn_vcw, L0_attn_vcb) + _L0_ffn_ref(xn, L0_ffn_gate, L0_ffn_W1, L0_ffn_b1, L0_ffn_W2, L0_ffn_b2)
    xn = _layernorm(x, axis=-1)
    x = x + _L1_attn_ref(xn, L1_attn_q1_w, L1_attn_q2_w, L1_attn_k1_w, L1_attn_k2_w, L1_attn_v_w, L1_attn_c_w, L1_attn_subln_w, L1_attn_lq1, L1_attn_lk1, L1_attn_lq2, L1_attn_lk2, L1_attn_bn_gamma, L1_attn_bn_beta) + _L1_ffn_ref(xn, L1_ffn_ln1_w, L1_ffn_ln1_b, L1_ffn_w_qkv, L1_ffn_w_proj, L1_ffn_ln2_w, L1_ffn_ln2_b, L1_ffn_gate_w, L1_ffn_gate_b, L1_ffn_w1, L1_ffn_w2)
    return x

_drawn_inputs = setup_inputs


def setup_inputs(seed=0):
    import zlib

    import numpy as np

    out = dict(_drawn_inputs(seed))
    spreads = {'L0_attn_ba': (2.0, 0.6),
     'L0_attn_bb': (0.0, 0.8),
     'L0_attn_rms_w': (1.0, 0.6),
     'L0_attn_qcb': (0.0, 0.1),
     'L0_attn_kcb': (0.0, 0.1),
     'L0_attn_vcb': (0.0, 0.1),
     'L0_ffn_b1': (0.0, 0.1),
     'L0_ffn_b2': (0.0, 0.1),
     'L1_attn_subln_w': (1.0, 0.542),
     'L1_attn_bn_gamma': (1.0, 0.2),
     'L1_attn_bn_beta': (0.0, 0.1),
     'L1_ffn_ln1_w': (1.0, 0.6),
     'L1_ffn_ln1_b': (0.0, 0.8),
     'L1_ffn_ln2_w': (1.0, 0.6),
     'L1_ffn_ln2_b': (0.0, 2.0),
     'L1_ffn_gate_b': (0.0, 2.0)}
    factors = {'L0_attn_Wa': 8.0,
     'L0_attn_Wb': 8.0,
     'L0_attn_Wgd': 8.0,
     'L0_attn_Wgu': 8.0,
     'L1_attn_lq1': 107.608,
     'L1_attn_lq2': 7.285,
     'L1_attn_lk2': 200.0,
     'L1_ffn_w_qkv': 8.0,
     'L1_ffn_w_proj': 8.0,
     'L1_attn_lk1': 35.28,
     'L1_ffn_gate_w': 3.712,
     'L1_ffn_w1': 3.096,
     'L1_ffn_w2': 3.11,
     'L1_attn_q1_w': 8.0,
     'L1_attn_k1_w': 8.0}
    for name, (base, spread) in spreads.items():
        noise = np.random.default_rng([zlib.crc32(name.encode()), seed]).standard_normal(out[name].shape)
        drawn = base * np.exp(spread * noise) if base else spread * noise
        out[name] = jnp.asarray(drawn.astype(out[name].dtype))
    for name, factor in factors.items():
        out[name] = (out[name] * factor).astype(out[name].dtype)
    return out
```

```python
import concourse.bass as bass
from concourse import mybir
import math
import numpy as np
from contextlib import ExitStack

F32 = mybir.dt.float32
BF16 = mybir.dt.bfloat16
ALU = mybir.AluOpType
ACT = mybir.ActivationFunctionType
AX_X = mybir.AxisListType.X

B, T, D = 8, 256, 128
P = 128
HALVES = T // P
NT = B * HALVES
H0, DK = 16, 8
C = 8
NC = T // C
HC = NC // HALVES
TAPS = 4
E0, F0 = 8, 256
PAD = TAPS - 1
LN_EPS = 1e-5


def layer0(nc, a, x1):
    with ExitStack() as ctx:
        def sb(name, shape, dt=F32):
            return ctx.enter_context(nc.sbuf_tensor(name, shape, dt))

        def sem(name):
            return ctx.enter_context(nc.semaphore(name))

        ps = [ctx.enter_context(nc.psum_tensor(f"l0_bank{i}", [P, 512], F32)) for i in range(8)]

        x = x1
        xn = sb("xn", [P, NT, D])
        stat = sb("stat", [P, HALVES, 4, B])
        xnT = sb("xnT", [P, B, PAD + T])
        ident = sb("ident", [P, P])
        ones = sb("ones", [1, P])
        w3 = sb("w3", [P, 3 * D + 40])
        wtap = sb("wtap", [P, PAD, 3 * D])
        bias = sb("bias", [1, 3 * D + 40])
        qkv = sb("qkv", [P, 3, B, D])
        raw = sb("raw", [P, 2, NT, H0])
        lg = sb("lg", [P, NT, E0])
        kb = sb("kb", [P, T, DK])
        qb = sb("qb", [P, T, DK])
        qt = sb("qt", [P, T, DK])
        kt = sb("kt", [P, T, DK])
        ab = sb("ab", [P, 2, T])
        nrm = sb("nrm", [P, 2, P])
        G = sb("G", [P, NC, C + 1])
        Dm = sb("Dm", [P, NC, C, C])
        KK = sb("KK", [P, HC, C, C])
        Y = sb("Y", [P, NC, C, 2 * DK])
        tmp = sb("tmp", [P, HC * 28 * DK])
        sq = tmp[:, 0:B * D].rearrange("p (b d) -> p b d", b=B)
        tmpo = sb("tmpo", [P, HC * 36 * DK])
        QK = sb("QK", [P, NC, C, C])
        S = sb("S", [P, NC + 1, DK, DK])
        U = Y[:, :, :, 0:DK]
        O = xn[:, :, :].rearrange("p m (h j) -> p (m h) j", j=DK)
        p1 = sb("p1", [P, C, DK, DK])
        r1 = sb("r1", [P, C, DK])
        p2 = sb("p2", [P, C + 1, DK, DK])
        wgd = sb("wgd", [P, 64])
        wgu = sb("wgu", [64, D])
        hT = sb("hT", [64, NT, P])
        gS = sb("gS", [P, NT, D])
        wo = sb("wo", [P, D])
        rmsw = sb("rmsw", [P, 1])
        W1 = sb("W1", [P, E0, F0])
        W2 = sb("W2", [P, E0 * 2, D])
        b1 = sb("b1", [P, E0 * 2])
        b2 = sb("b2", [E0, D])
        gw = sb("gw", [P, NT, E0])
        qkv_flat = qkv[:, :, :, :].rearrange("p n b c -> p (n b c)")
        gs = qkv_flat[:, 0:6 * NT * E0].rearrange("p (k m e) -> p k m e", k=6, e=E0)
        yg = qkv_flat[:, 1024:1024 + 8 * D].rearrange("p (u i d) -> p u i d", u=2, i=4)
        gm = sb("gm", [P, NT])
        iota8 = sb("iota8", [P, E0])
        gwT = hT[0:E0, :, :]
        hS = sb("hS", [P, 2, 2, 512])
        nsq = hS[:, :, :, :].rearrange("p a b t -> p (a b t)").rearrange("p (w t i) -> p w t i", w=2, i=DK)
        cw = hS[:, :, :, :].rearrange("p a b t -> p (a b t)")[:, 0:3 * D * TAPS].rearrange("p (c k) -> p c k", k=TAPS)

        ld_x = [sem(f"ld_x{f}") for f in range(HALVES)]
        ld_w, ld_cw, ld_g, ld_moe = sem("ld_w"), sem("ld_cw"), sem("ld_g"), sem("ld_moe")
        s_const = sem("s_const")
        s_centred, s_squared, s_var, s_std, s_xn = (sem(n) for n in ("s_centred", "s_squared", "s_var", "s_std", "s_xn"))
        s_xT_ps, s_xnT = sem("s_xT_ps"), sem("s_xnT")
        s_wtap = sem("s_wtap")
        s_proj, s_silu, s_raw, s_ab = sem("s_proj"), sem("s_silu"), sem("s_raw"), sem("s_ab")
        s_bh_ps, s_bhA, s_bhV = sem("s_bh_ps"), sem("s_bhA"), sem("s_bhV")
        s_nsq, s_n2, s_nrm, s_kq = sem("s_nsq"), sem("s_n2"), sem("s_nrm"), sem("s_kq")
        s_decay = sem("s_decay")
        s_h_ps, s_hT, s_g_ps, s_g = sem("s_h_ps"), sem("s_hT"), sem("s_g_ps"), sem("s_g")
        s_gexp, s_gshift, s_gw, s_gwT_ps, s_gwT = sem("s_gexp"), sem("s_gshift"), sem("s_gw"), sem("s_gwT_ps"), sem("s_gwT")
        s_up, s_relu, s_down, s_yg, s_acc = sem("s_up"), sem("s_relu"), sem("s_down"), sem("s_yg"), sem("s_acc")
        s_qk, s_chain, s_intra, s_O = sem("s_qk"), sem("s_chain"), sem("s_intra"), sem("s_O")
        s_O_ps, s_Ot, s_Osq, s_Ovar, s_Ostd, s_Og = (sem(n) for n in ("s_O_ps", "s_Ot", "s_Osq", "s_Ovar", "s_Ostd", "s_Og"))
        s_OT_ps, s_OT, s_wo, s_out_ps, s_x1 = (sem(n) for n in ("s_OT_ps", "s_OT", "s_wo", "s_out_ps", "s_x1"))
        s_dve, s_pool, s_act = sem("s_dve"), sem("s_pool"), sem("s_act")
        Ot = kb[:, :, :].rearrange("p (m h) j -> p m (h j)", h=H0)
        OT = xn
        acc = x

        block = ctx.enter_context(nc.Block())
        tok = lambda ap: ap.rearrange("b (f p) d -> p f b d", p=P)

        BH = [("k", 0, "V"), ("k", 4, "A"), ("q", 0, "V"), ("q", 4, "A"), ("ab", 0, "V"), ("v", 0, "V"), ("v", 4, "A")]
        COL = {"q": 0, "k": 1, "v": 2}
        NBH = len(BH)

        def bh_group(n):
            return n // NBH, BH[n % NBH]

        def bh_evacuated(n):
            v = sum(bh_group(k)[1][2] == "V" for k in range(n))
            return n - v, v

        def bh_dst(f, t, i0):
            rows = slice(f * P, f * P + P)
            if t == "k":
                return kb[:, rows, i0:i0 + 4]
            if t == "q":
                return qb[:, rows, i0:i0 + 4]
            return Y[:, f * HC:(f + 1) * HC, :, i0:i0 + 4].rearrange("p c t i -> p (c t) i")

        @block.sync
        def _(sp):
            for f in range(HALVES):
                sp.dma_start(x[:, f * B:(f + 1) * B, :], tok(a["L0_attn_x"])[:, f]).then_inc(ld_x[f], 16)
            for n, name in enumerate(("L0_attn_qcw", "L0_attn_kcw", "L0_attn_vcw")):
                sp.dma_start(cw[:, n * D:(n + 1) * D, :], a[name].partition_broadcast(P)).then_inc(ld_cw, 16)
            for n, name in enumerate(("L0_attn_Wgd", )):
                sp.dma_start(wgd[:, :], a[name]).then_inc(ld_g, 16)
            sp.dma_start(wgu[:, :], a["L0_attn_Wgu"]).then_inc(ld_g, 16)
            sp.dma_start(W1[:, :, :], a["L0_ffn_W1"].rearrange("e d h -> d e h")).then_inc(ld_moe, 16)
            sp.dma_start(W2[:, :, :], a["L0_ffn_W2"].rearrange("e (c p) d -> p (e c) d", p=P)).then_inc(ld_moe, 16)
            sp.dma_start(b1[:, :], a["L0_ffn_b1T"]).then_inc(ld_moe, 16)
            sp.dma_start(b2[:, :], a["L0_ffn_b2"]).then_inc(ld_moe, 16)

        @block.gpsimd
        def _(pool):
            V = nc.gpsimd
            n = 0

            def chain(ins):
                nonlocal n
                ins.then_inc(s_pool, 1)
                n += 1
                pool.wait_ge(s_pool, n)

            chain(V.memset(ident[:, :], 0.0))
            V.affine_select(out=ident[:, :], in_=ident[:, :], compare_op=ALU.not_equal, fill=1.0, base=0,
                            pattern=[[-1, P]], channel_multiplier=1).then_inc(s_const, 1)
            V.memset(ones[:, :], 1.0).then_inc(s_const, 1)
            V.memset(bias[:, 3 * D + 32:3 * D + 40], 0.0).then_inc(s_const, 1)
            V.memset(xnT[:, :, 0:PAD], 0.0).then_inc(s_const, 1)
            for e in range(E0):
                V.memset(iota8[:, e:e + 1], float(E0 - e)).then_inc(s_const, 1)
            V.memset(Dm[:, :, :, :], 0.0).then_inc(s_const, 1)
            V.memset(KK[:, :, :, :], 0.0).then_inc(s_const, 1)
            V.memset(QK[:, :, :, :], 0.0).then_inc(s_const, 1)
            V.memset(G[:, :, 0:1], 1.0).then_inc(s_const, 1)
            V.memset(S[:, 0, :, :], 0.0).then_inc(s_const, 1)
            pool.wait_ge(s_const, CONSTS)
            pool.wait_ge(ld_w, 16 * LDW)
            pool.wait_ge(ld_cw, 48)
            for k in range(PAD):
                V.tensor_tensor(wtap[:, k, :], w3[:, 0:3 * D], cw[:, :, k], ALU.mult).then_inc(s_wtap, 1)
            pool.wait_ge(s_wtap, PAD)
            V.tensor_tensor(w3[:, 0:3 * D], w3[:, 0:3 * D], cw[:, :, PAD], ALU.mult).then_inc(s_wtap, 1)

            def decays(f):
                cs = slice(f * HC, (f + 1) * HC)
                al = ab[:, 0, f * P:(f + 1) * P].rearrange("p (c t) -> p c t", t=C)
                be = ab[:, 1, f * P:(f + 1) * P].rearrange("p (c t) -> p c t", t=C)
                diag = Dm[:, cs, :, :].rearrange("p c t s -> p c (t s)")[:, :, 0:C * C:C + 1]
                pool.wait_ge(s_bhV, bh_evacuated(f * NBH + 5)[1])
                chain(V.tensor_copy(diag, be))
                for t in range(C):
                    if t:
                        V.tensor_tensor(Dm[:, cs, t, 0:t], Dm[:, cs, t - 1, 0:t],
                                        al[:, :, t:t + 1].to_broadcast([P, HC, t]), ALU.mult).then_inc(s_pool, 1)
                        step()
                    chain(V.tensor_tensor(G[:, cs, t + 1], G[:, cs, t], al[:, :, t], ALU.mult))

            def step():
                nonlocal n
                n += 1

            def queries(f):
                cs = slice(f * HC, (f + 1) * HC)
                k3 = kb[:, f * P:(f + 1) * P, :].rearrange("p (c t) i -> p c t i", t=C)
                q3 = qb[:, f * P:(f + 1) * P, :].rearrange("p (c t) i -> p c t i", t=C)
                pool.wait_ge(s_kq, 2 * f + 2)
                off = 0
                for s in range(C):
                    m = C - s
                    dst = tmpo[:, off:off + HC * m * DK].rearrange("p (c t i) -> p c t i", c=HC, t=m)
                    V.tensor_tensor(dst, q3[:, :, s:C, :], k3[:, :, s:s + 1, :].to_broadcast([P, HC, m, DK]),
                                    ALU.mult).then_inc(s_pool, 1)
                    step()
                    off += HC * m * DK
                pool.wait_ge(s_pool, n)
                all8 = tmpo[:, 0:off].rearrange("p (x i) -> p x i", i=DK)
                chain(V.tensor_tensor(all8[:, :, 0:4], all8[:, :, 0:4], all8[:, :, 4:8], ALU.add))
                chain(V.tensor_tensor(all8[:, :, 0:2], all8[:, :, 0:2], all8[:, :, 2:4], ALU.add))
                off = 0
                for s in range(C):
                    m = C - s
                    t3 = tmpo[:, off:off + HC * m * DK].rearrange("p (c t i) -> p c t i", c=HC, t=m)
                    V.tensor_tensor(QK[:, cs, s:C, s], t3[:, :, :, 0], t3[:, :, :, 1], ALU.add).then_inc(s_pool, 1)
                    step()
                    off += HC * m * DK
                pool.wait_ge(s_pool, n)
                V.tensor_tensor(QK[:, cs, :, :], QK[:, cs, :, :], Dm[:, cs, :, :], ALU.mult).then_inc(s_qk, 1)

            def mixture(g):
                for q in range(2):
                    for j in range(4):
                        m, u = g * 4 + j, g * 8 + q * 4 + j
                        pool.wait_ge(s_yg, 4 * (u + 1))
                        v = yg[:, u % 2, :, :]
                        chain(V.tensor_tensor(v[:, 0:2, :], v[:, 0:2, :], v[:, 2:4, :], ALU.add))
                        if q:
                            chain(V.tensor_tensor(v[:, 0, :], v[:, 0, :], v[:, 1, :], ALU.add))
                            V.tensor_tensor(acc[:, m, :], acc[:, m, :], v[:, 0, :], ALU.add).then_inc(s_acc, 1)
                        else:
                            chain(V.tensor_tensor(v[:, 0, :], v[:, 0, :], v[:, 1, :], ALU.add))
                            V.tensor_tensor(acc[:, m, :], x[:, m, :], v[:, 0, :], ALU.add).then_inc(s_acc, 1)
                pool.wait_ge(s_acc, 8 * (g + 1))

            def intra(f):
                pool.wait_ge(s_chain, f + 1)
                pool.wait_ge(s_qk, f + 1)
                cs = slice(f * HC, (f + 1) * HC)
                o3 = O[:, f * P:(f + 1) * P, :].rearrange("p (c t) j -> p c t j", t=C)
                for s in range(C):
                    m = C - s
                    dst = o3 if s == 0 else tmpo[:, 0:HC * m * DK].rearrange("p (c t i) -> p c t i", c=HC, t=m)
                    chain(V.tensor_tensor(dst, QK[:, cs, s:C, s].unsqueeze(3).to_broadcast([P, HC, m, DK]),
                                          U[:, cs, s:s + 1, :].to_broadcast([P, HC, m, DK]), ALU.mult))
                    if s:
                        chain(V.tensor_tensor(o3[:, :, s:C, :], o3[:, :, s:C, :], dst, ALU.add))
                pool.nop().then_inc(s_intra, 1)

            decays(0)
            pool.nop().then_inc(s_decay, 1)
            queries(0)
            decays(1)
            pool.nop().then_inc(s_decay, 1)
            queries(1)
            mixture(0)
            mixture(1)
            intra(0)
            mixture(2)
            mixture(3)

        @block.scalar
        def _(act):
            A = nc.scalar
            for n, name in enumerate(("L0_attn_Wq", "L0_attn_Wk", "L0_attn_Wv")):
                act.dma_start(w3[:, n * D:(n + 1) * D], a[name]).then_inc(ld_w, 16)
                act.dma_start(bias[:, n * D:(n + 1) * D], a["L0_attn_" + "qkv"[n] + "cb"].unsqueeze(0)).then_inc(ld_w, 16)
            for n, name in enumerate(("L0_attn_Wa", "L0_attn_Wb", "L0_ffn_gate")):
                w = a[name].shape[1]
                act.dma_start(w3[:, 3 * D + 16 * n:3 * D + 16 * n + w], a[name]).then_inc(ld_w, 16)
            act.dma_start(bias[:, 3 * D:3 * D + 16], a["L0_attn_ba"].unsqueeze(0)).then_inc(ld_w, 16)
            act.dma_start(bias[:, 3 * D + 16:3 * D + 32], a["L0_attn_bb"].unsqueeze(0)).then_inc(ld_w, 16)
            act.dma_start(wo[:, :], a["L0_attn_Wo"]).then_inc(ld_g, 16)
            act.dma_start(rmsw[:, :], a["L0_attn_rms_w"].rearrange("h (j o) -> (h j) o", o=1)).then_inc(ld_g, 16)
            for f in range(HALVES):
                act.wait_ge(s_centred, f + 1)
                if f:
                    act.wait_ge(s_var, f)
                A.activation(sq[:, :, :], xn[:, f * B:(f + 1) * B, :], ACT.Square).then_inc(s_squared, 1)
                act.wait_ge(s_var, f + 1)
                A.activation(stat[:, f, 2, :], stat[:, f, 1, :], ACT.Sqrt).then_inc(s_std, 1)
            for g in range(4):
                act.wait_ge(s_xT_ps, g + 1)
                if g == 0:
                    act.wait_ge(s_const, CONSTS)
                f, b0 = g // 2, (g % 2) * 4
                A.activation(xnT[:, b0:b0 + 4, PAD + f * P:PAD + (f + 1) * P],
                             ps[g][:, :].rearrange("p (b t) -> p b t", b=4), ACT.Copy).then_inc(s_xnT, 1)

            def half(f):
                for m in range(f * B, (f + 1) * B):
                    act.wait_ge(s_proj, m + 1)
                    if m == B:
                        act.wait_ge(s_bh_ps, NBH)
                    A.activation(qkv[:, :, m % B, :], ps[4 + m % 4][:, 0:3 * D].rearrange("p (n d) -> p n d", d=D),
                                 ACT.Silu).then_inc(s_silu, 1)
                for g in range(2):
                    act.wait_ge(s_h_ps, 2 * f + g + 1)
                    A.activation(hT[:, f * B + g * 4:f * B + g * 4 + 4, :].rearrange("p m t -> p (m t)"),
                                 ps[g][0:64, :], ACT.Silu).then_inc(s_hT, 1)
                act.wait_ge(s_raw, 2 * (f + 1) * B)
                ab_half = raw[:, :, f * B:(f + 1) * B, :]
                A.activation(ab_half, ab_half, ACT.Sigmoid).then_inc(s_ab, 1)
                for n in range(f * NBH, (f + 1) * NBH):
                    _, (t, i0, who) = bh_group(n)
                    if who == "A":
                        act.wait_ge(s_bh_ps, n + 1)
                        A.activation(bh_dst(f, t, i0), ps[n % 4][:, :].rearrange("p (i t) -> p t i", i=4),
                                     ACT.Copy).then_inc(s_bhA, 1)
                    if (t, i0) in (("k", 4), ("q", 4)):
                        w = 0 if t == "k" else 1
                        act.wait_ge(s_bhA, bh_evacuated(n + 1)[0])
                        act.wait_ge(s_bhV, bh_evacuated(n + 1)[1])
                        if f:
                            act.wait_ge(s_n2, 2 * f)
                        A.activation(nsq[:, w, :, :], (kb, qb)[w][:, f * P:(f + 1) * P, :], ACT.Square).then_inc(s_nsq, 1)
                act.wait_ge(s_n2, 2 * f + 2)
                if f:
                    act.wait_ge(s_kq, 2 * f)
                A.activation(nrm[:, :, :], nrm[:, :, :], ACT.Sqrt).then_inc(s_nrm, 1)
                for g in range(2):
                    act.wait_ge(s_g_ps, 2 * f + g + 1)
                    A.activation(gS[:, f * B + g * 4:f * B + g * 4 + 4, :].rearrange("p m d -> p (m d)"),
                                 ps[4 + g][:, :], ACT.Sigmoid).then_inc(s_g, 1)

            half(0)
            half(1)
            act.wait_ge(s_gshift, 1)
            A.activation(gs[:, 1, :, :], gs[:, 0, :, :], ACT.Exp).then_inc(s_gexp, 1)
            for g in range(4):
                act.wait_ge(s_gwT_ps, g + 1)
                A.activation(gwT[:, g * 4:g * 4 + 4, :].rearrange("p m t -> p (m t)"), ps[6 + g % 2][0:E0, :],
                             ACT.Copy).then_inc(s_gwT, 1)
            act.wait_ge(ld_moe, 64)
            for g in range(4):
                for e in range(E0):
                    for c in range(2):
                        u = (g * E0 + e) * 2 + c
                        act.wait_ge(s_up, u + 1)
                        if u >= 4:
                            act.wait_ge(s_down, (u - 4) // 2 + 1)
                        A.activation(hS[:, (u // 2) % 2, c, :], ps[c][:, :], ACT.Relu,
                                     bias=b1[:, 2 * e + c:2 * e + c + 1]).then_inc(s_relu, 1)
                    if e % 4 == 3:
                        act.wait_ge(s_down, g * E0 + e + 1)
                        for j in range(4):
                            u = (g * 2 + e // 4) * 4 + j
                            if u >= 2:
                                act.wait_ge(s_acc, u - 1)
                            for i in range(4):
                                A.activation(yg[:, u % 2, i, :], ps[4 + j][:, i * D:(i + 1) * D], ACT.Copy,
                                             scale=gw[:, g * 4 + j, e - 3 + i:e - 2 + i]).then_inc(s_yg, 1)
            for g in range(4):
                f = g // 2
                act.wait_ge(s_O_ps, g + 1)
                if g % 2 == 1:
                    A.activation(Ot[:, f * B:(f + 1) * B, :].rearrange("p m (h j) -> p m h j", j=DK)[:, :, :, 4:8],
                                 ps[g][:, :].rearrange("p (j m h) -> p m h j", j=4, h=H0), ACT.Copy).then_inc(s_Ot, 1)
            for f in range(HALVES):
                act.wait_ge(s_Ot, 4)
                if f:
                    act.wait_ge(s_Ovar, f)
                A.activation(sq[:, :, :], Ot[:, f * B:(f + 1) * B, :], ACT.Square).then_inc(s_Osq, 1)
            for f in range(HALVES):
                act.wait_ge(s_Ovar, f + 1)
                A.activation(nrm[:, f, :], nrm[:, f, :], ACT.Sqrt).then_inc(s_Ostd, 1)
            for g in range(4):
                act.wait_ge(s_OT_ps, g + 1)
                A.activation(OT[:, g * 4:g * 4 + 4, :].rearrange("p m t -> p (m t)"), ps[4 + g][:, :],
                             ACT.Copy).then_inc(s_OT, 1)

        @block.vector
        def _(dve):
            V = nc.vector
            n = 0

            def link(ins):
                nonlocal n
                ins.then_inc(s_dve, 1)
                n += 1
                dve.wait_ge(s_dve, n)

            def free(ins):
                nonlocal n
                ins.then_inc(s_dve, 1)
                n += 1

            def settle():
                dve.wait_ge(s_dve, n)

            def bc(ap, shape):
                return ap.to_broadcast(shape)

            hx = [slice(f * B, (f + 1) * B) for f in range(HALVES)]
            for f in range(HALVES):
                dve.wait_ge(ld_x[f], 16)
                link(V.tensor_reduce(stat[:, f, 0, :], x[:, hx[f], :], AX_X, ALU.add))
                link(V.tensor_scalar(stat[:, f, 0, :], stat[:, f, 0, :], 1.0 / D, None, ALU.mult))
                V.tensor_tensor(xn[:, hx[f], :], x[:, hx[f], :], bc(stat[:, f, 0, :].unsqueeze(2), [P, B, D]),
                                ALU.subtract).then_inc(s_centred, 1)
            for f in range(HALVES):
                dve.wait_ge(s_squared, f + 1)
                link(V.tensor_reduce(stat[:, f, 1, :], sq[:, :, :], AX_X, ALU.add))
                V.tensor_scalar(stat[:, f, 1, :], stat[:, f, 1, :], 1.0 / D, LN_EPS, ALU.mult, ALU.add).then_inc(s_var, 1)
                dve.wait_ge(s_std, f + 1)
                link(V.reciprocal(stat[:, f, 3, :], stat[:, f, 2, :]))
                V.tensor_tensor(xn[:, hx[f], :], xn[:, hx[f], :], bc(stat[:, f, 3, :].unsqueeze(2), [P, B, D]),
                                ALU.mult).then_inc(s_xn, 1)

            def gather(f):
                for m in range(f * B, (f + 1) * B):
                    dve.wait_ge(s_silu, m + 1)
                    bank = ps[4 + m % 4]
                    V.tensor_copy(raw[:, :, m, :], bank[:, 3 * D:3 * D + 32].rearrange("p (w h) -> p w h", w=2)).then_inc(s_raw, 1)
                    V.tensor_copy(lg[:, m, :], bank[:, 3 * D + 32:3 * D + 40]).then_inc(s_raw, 1)
                for g in range(f * NBH, (f + 1) * NBH):
                    _, (t, i0, who) = bh_group(g)
                    if who != "V":
                        continue
                    dve.wait_ge(s_bh_ps, g + 1)
                    src = ps[g % 4][:, :]
                    if t == "ab":
                        dst = ab[:, :, f * P:(f + 1) * P]
                        link(V.tensor_scalar(dst[:, 0], src[:, 0:P], 0.1, 1.0, ALU.max, ALU.min))
                        V.tensor_scalar(dst[:, 1], src[:, P:2 * P], 1.0, None, ALU.min).then_inc(s_bhV, 1)
                    else:
                        V.tensor_copy(bh_dst(f, t, i0), src.rearrange("p (i t) -> p t i", i=4)).then_inc(s_bhV, 1)
                for w in range(2):
                    dve.wait_ge(s_nsq, 2 * f + w + 1)
                    V.tensor_reduce(nrm[:, w, :], nsq[:, w, :, :], AX_X, ALU.add).then_inc(s_n2, 1)
                dve.wait_ge(s_nrm, f + 1)
                link(V.tensor_scalar(nrm[:, :, :], nrm[:, :, :], 1e-6, None, ALU.max))
                link(V.reciprocal(nrm[:, :, :], nrm[:, :, :]))
                for w in range(2):
                    z = (kb, qb)[w][:, f * P:(f + 1) * P, :]
                    V.tensor_tensor(z, z, bc(nrm[:, w, :].unsqueeze(2), [P, P, DK]), ALU.mult).then_inc(s_kq, 1)
                dve.wait_ge(s_kq, 2 * f + 2)

            def solve(f):
                cs = slice(f * HC, (f + 1) * HC)
                k3 = kb[:, f * P:(f + 1) * P, :].rearrange("p (c t) i -> p c t i", t=C)
                q3 = qb[:, f * P:(f + 1) * P, :].rearrange("p (c t) i -> p c t i", t=C)
                off = 0
                for s in range(C - 1):
                    m = C - 1 - s
                    t3 = tmp[:, off:off + HC * m * DK].rearrange("p (c t i) -> p c t i", c=HC, t=m)
                    free(V.tensor_tensor(t3, k3[:, :, s + 1:C, :], bc(k3[:, :, s:s + 1, :], [P, HC, m, DK]), ALU.mult))
                    off += HC * m * DK
                settle()
                off = 0
                for s in range(C - 1):
                    m = C - 1 - s
                    t3 = tmp[:, off:off + HC * m * DK].rearrange("p (c t i) -> p c t i", c=HC, t=m)
                    free(V.tensor_reduce(KK[:, :, s + 1:C, s], t3, AX_X, ALU.add))
                    off += HC * m * DK
                dve.wait_ge(s_decay, f + 1)
                y4 = Y[:, cs, :, :]
                free(V.tensor_tensor(y4[:, :, :, DK:2 * DK], k3, bc(G[:, cs, 0:C].unsqueeze(3), [P, HC, C, DK]), ALU.mult))
                free(V.tensor_tensor(kt[:, f * P:(f + 1) * P, :].rearrange("p (c t) i -> p c t i", t=C), k3,
                                     bc(Dm[:, cs, C - 1, :].unsqueeze(3), [P, HC, C, DK]), ALU.mult))
                free(V.tensor_tensor(qt[:, f * P:(f + 1) * P, :].rearrange("p (c t) i -> p c t i", t=C), q3,
                                     bc(G[:, cs, 1:C + 1].unsqueeze(3), [P, HC, C, DK]), ALU.mult))
                settle()
                link(V.tensor_tensor(KK[:, :, 1:C, :], KK[:, :, 1:C, :], Dm[:, cs, 0:C - 1, :], ALU.mult))
                dve.wait_ge(s_bhA, bh_evacuated((f + 1) * NBH)[0])
                for s in range(C - 1):
                    m = C - 1 - s
                    t3 = tmp[:, 0:HC * m * 2 * DK].rearrange("p (c t i) -> p c t i", c=HC, t=m)
                    link(V.tensor_tensor(t3, bc(KK[:, :, s + 1:C, s].unsqueeze(3), [P, HC, m, 2 * DK]),
                                         bc(y4[:, :, s:s + 1, :], [P, HC, m, 2 * DK]), ALU.mult))
                    link(V.tensor_tensor(y4[:, :, s + 1:C, :], y4[:, :, s + 1:C, :], t3, ALU.subtract))

            def recur(f):
                ktc = kt[:, :, :].rearrange("p (c t) i -> p c t i", t=C)
                for c in range(f * HC, (f + 1) * HC):
                    full = [P, C, DK, DK]
                    free(V.tensor_tensor(p1[:, :, :, :], bc(Y[:, c, :, DK:2 * DK].unsqueeze(2), full),
                                         bc(S[:, c, :, :].unsqueeze(1), full), ALU.mult))
                    m1 = n
                    free(V.tensor_scalar(p2[:, C, :, :], S[:, c, :, :], G[:, c, C:C + 1], None, ALU.mult))
                    dve.wait_ge(s_dve, m1)
                    link(V.tensor_reduce(r1[:, :, :], p1[:, :, :, :], AX_X, ALU.add))
                    link(V.tensor_tensor(U[:, c, :, :], Y[:, c, :, 0:DK], r1[:, :, :], ALU.subtract))
                    link(V.tensor_tensor(p2[:, 0:C, :, :], bc(U[:, c, :, :].unsqueeze(3), full),
                                         bc(ktc[:, c, :, :].unsqueeze(2), full), ALU.mult))
                    link(V.tensor_reduce(S[:, c + 1, :, :], p2[:, :, :, :].rearrange("p t j i -> p j i t"), AX_X, ALU.add))
                V.tensor_copy(p1[:, 0, 0, 0:1], S[:, 0, 0, 0:1]).then_inc(s_chain, 1)

            def router():
                full = [P, NT, E0]
                link(V.tensor_reduce(gm[:, :], lg[:, :, :], AX_X, ALU.max))
                V.tensor_tensor(gs[:, 0], lg[:, :, :], bc(gm[:, :].unsqueeze(2), full), ALU.subtract).then_inc(s_gshift, 1)
                dve.wait_ge(s_gexp, 1)
                link(V.tensor_reduce(gm[:, :], gs[:, 1], AX_X, ALU.add))
                link(V.reciprocal(gm[:, :], gm[:, :]))
                link(V.tensor_tensor(gs[:, 1], gs[:, 1], bc(gm[:, :].unsqueeze(2), full), ALU.mult))
                link(V.tensor_copy(gs[:, 2], gs[:, 1]))
                io = bc(iota8[:, :].unsqueeze(1), full)
                for k in range(2):
                    link(V.tensor_reduce(gm[:, :], gs[:, 2], AX_X, ALU.max))
                    link(V.tensor_tensor(gs[:, 3], gs[:, 2], bc(gm[:, :].unsqueeze(2), full), ALU.is_equal))
                    link(V.tensor_tensor(gs[:, 3], gs[:, 3], io, ALU.mult))
                    link(V.tensor_reduce(gm[:, :], gs[:, 3], AX_X, ALU.max))
                    link(V.tensor_tensor(gs[:, 4 + k], gs[:, 3], bc(gm[:, :].unsqueeze(2), full), ALU.is_equal))
                    if k == 0:
                        link(V.tensor_tensor(gs[:, 2], gs[:, 2], gs[:, 4], ALU.subtract))
                        link(V.tensor_tensor(gs[:, 2], gs[:, 2], gs[:, 4], ALU.subtract))
                link(V.tensor_tensor(gs[:, 4], gs[:, 4], gs[:, 5], ALU.add))
                link(V.tensor_tensor(gs[:, 4], gs[:, 4], gs[:, 1], ALU.mult))
                link(V.tensor_reduce(gm[:, :], gs[:, 4], AX_X, ALU.add))
                link(V.tensor_scalar(gm[:, :], gm[:, :], 1e-12, None, ALU.max))
                link(V.reciprocal(gm[:, :], gm[:, :]))
                V.tensor_tensor(gw[:, :, :], gs[:, 4], bc(gm[:, :].unsqueeze(2), full), ALU.mult).then_inc(s_gw, 1)

            def inter(f):
                qc = qt[:, :, :].rearrange("p (c t) i -> p t c i", t=C)[:, :, f * HC:(f + 1) * HC, :]
                cs = slice(f * HC, (f + 1) * HC)
                full = [P, HC, DK, DK]
                for t in range(C):
                    buf = tmp[:, (t % 2) * 1024:(t % 2) * 1024 + 1024].rearrange("p (c j i) -> p c j i", c=HC, j=DK)
                    link(V.tensor_tensor(buf, bc(qc[:, t].unsqueeze(2), full), S[:, cs, :, :], ALU.mult))
                    free(V.tensor_reduce(tmp2[:, :, t, :], buf, AX_X, ALU.add))
                settle()
                o = O[:, f * P:(f + 1) * P, :]
                V.tensor_tensor(o, o, tmp2.rearrange("p c t j -> p (c t) j"), ALU.add).then_inc(s_O, 1)

            tmp2 = tmp[:, 2048:3072].rearrange("p (c t j) -> p c t j", c=HC, t=C)
            dve.wait_ge(s_const, CONSTS)
            gather(0)
            solve(0)
            gather(1)
            router()
            recur(0)
            solve(1)
            recur(1)
            dve.wait_ge(s_intra, 1)
            inter(0)
            dve.wait_ge(s_qk, 2)
            cs = slice(HC, 2 * HC)
            o3 = O[:, P:2 * P, :].rearrange("p (c t) j -> p c t j", t=C)
            for s in range(C):
                m = C - s
                dst = o3 if s == 0 else tmp[:, 0:HC * m * DK].rearrange("p (c t i) -> p c t i", c=HC, t=m)
                link(V.tensor_tensor(dst, bc(QK[:, cs, s:C, s].unsqueeze(3), [P, HC, m, DK]),
                                     bc(U[:, cs, s:s + 1, :], [P, HC, m, DK]), ALU.mult))
                if s:
                    link(V.tensor_tensor(o3[:, :, s:C, :], o3[:, :, s:C, :], dst, ALU.add))
            inter(1)
            dve.wait_ge(ld_g, 64)
            V.tensor_scalar(wo[:, :], wo[:, :], rmsw[:, 0:1], None, ALU.mult).then_inc(s_wo, 1)
            for g in range(0, 4, 2):
                f = g // 2
                dve.wait_ge(s_O_ps, g + 1)
                V.tensor_copy(Ot[:, f * B:(f + 1) * B, :].rearrange("p m (h j) -> p m h j", j=DK)[:, :, :, 0:4],
                              ps[g][:, :].rearrange("p (j m h) -> p m h j", j=4, h=H0)).then_inc(s_Ot, 1)
            dve.wait_ge(s_g, 4)
            for f in range(HALVES):
                dve.wait_ge(s_Osq, f + 1)
                link(V.tensor_reduce(nrm[:, f, :], sq[:, :, :].rearrange("p m (h j) -> p (m h) j", j=DK), AX_X, ALU.add))
                V.tensor_scalar(nrm[:, f, :], nrm[:, f, :], 1.0 / DK, 1e-6, ALU.mult, ALU.add).then_inc(s_Ovar, 1)
                link(V.tensor_tensor(Ot[:, hx[f], :], Ot[:, hx[f], :], gS[:, hx[f], :], ALU.mult))
            for f in range(HALVES):
                dve.wait_ge(s_Ostd, f + 1)
                link(V.reciprocal(nrm[:, f, :], nrm[:, f, :]))
                o = Ot[:, hx[f], :].rearrange("p m (h j) -> p m h j", j=DK)
                V.tensor_tensor(o, o, bc(nrm[:, f, :].rearrange("p (m h) -> p m h", h=H0).unsqueeze(3), [P, B, H0, DK]),
                                ALU.mult).then_inc(s_Og, 1)
            dve.wait_ge(s_acc, 32)
            for g in range(4):
                dve.wait_ge(s_out_ps, g + 1)
                V.tensor_tensor(x1[:, 4 * g:4 * g + 4, :].rearrange("p m d -> p (m d)"), ps[g][:, :],
                                acc[:, 4 * g:4 * g + 4, :].rearrange("p m d -> p (m d)"), ALU.add).then_inc(s_x1, 1)
            dve.wait_ge(s_x1, 4)

        @block.tensor
        def _(pe):
            M = nc.tensor
            pe.wait_ge(s_const, CONSTS)
            for f in range(HALVES):
                pe.wait_ge(s_xn, f + 1)
                for b in range(B):
                    g = f * 2 + b // 4
                    last = M.transpose(ps[g][:, (b % 4) * P:(b % 4 + 1) * P], xn[:, f * B + b, :], ident[:, :])
                    if b % 4 == 3:
                        last.then_inc(s_xT_ps, 1)

            def projections(f):
                pe.wait_ge(s_xnT, 2 * f + 2)
                if f == 0:
                    pe.wait_ge(s_wtap, PAD + 1)
                    pe.wait_ge(ld_w, 16 * LDW)
                for b in range(B):
                    m = f * B + b
                    if m >= 4:
                        pe.wait_ge(s_silu, m - 3)
                        pe.wait_ge(s_raw, 2 * (m - 3))
                    if m == B:
                        pe.wait_ge(s_g, 2)
                    bank = ps[4 + m % 4]
                    M.matmul(bank[:, 0:3 * D + 40], ones[:, :], bias[:, :], start=True, stop=False)
                    for k in range(PAD):
                        M.matmul(bank[:, 0:3 * D], xnT[:, b, f * P + k:f * P + k + P], wtap[:, k, :],
                                 start=False, stop=False)
                    M.matmul(bank[:, 0:3 * D + 40], xnT[:, b, f * P + PAD:f * P + PAD + P], w3[:, :],
                             start=False, stop=True).then_inc(s_proj, 1)

            def xT(g):
                f, b0 = g // 2, (g % 2) * 4
                return xnT[:, b0:b0 + 4, PAD + f * P:PAD + (f + 1) * P]

            def gate_hidden(f):
                if f == 0:
                    pe.wait_ge(ld_g, 64)
                    pe.wait_ge(s_xnT, 4)
                else:
                    pe.wait_ge(s_bhA, bh_evacuated(NBH)[0])
                    pe.wait_ge(s_bhV, bh_evacuated(NBH)[1])
                for g in range(2):
                    M.matmul(ps[g][0:64, :], wgd[:, :], xT(2 * f + g), start=True, stop=True).then_inc(s_h_ps, 1)

            def gate_out(f):
                for g in range(2):
                    pe.wait_ge(s_hT, 2 * f + g + 1)
                    pe.wait_ge(s_silu, (f + 1) * B)
                    pe.wait_ge(s_raw, 2 * (f + 1) * B)
                    for j in range(4):
                        last = M.matmul(ps[4 + g][:, j * D:(j + 1) * D], hT[:, f * B + g * 4 + j, :], wgu[:, :],
                                        start=True, stop=True)
                    last.then_inc(s_g_ps, 1)

            def heads(f):
                pe.wait_ge(s_silu, (f + 1) * B)
                pe.wait_ge(s_ab, f + 1)
                pe.wait_ge(s_hT, 2 * f + 2)
                for n in range(f * NBH, (f + 1) * NBH):
                    _, (t, i0, who) = bh_group(n)
                    if n % NBH >= 4:
                        na, nv = bh_evacuated(n - 3)
                        pe.wait_ge(s_bhA, na)
                        pe.wait_ge(s_bhV, nv)
                    elif n >= 4:
                        pe.wait_ge(s_bhA, bh_evacuated(NBH)[0])
                        pe.wait_ge(s_bhV, bh_evacuated(NBH)[1])
                    for j in range(2 if t == "ab" else 4):
                        if t == "ab":
                            src = raw[:, j, f * B:(f + 1) * B, :].rearrange("p m h -> p (m h)")
                        else:
                            src = qkv[:, COL[t], :, :].rearrange("p b c -> p (b c)")[:, i0 + j:B * D:DK]
                        last = M.transpose(ps[n % 4][:, j * P:(j + 1) * P], src, ident[:, :])
                    last.then_inc(s_bh_ps, 1)

            projections(0)
            gate_hidden(0)
            heads(0)
            gate_out(0)
            projections(1)
            gate_hidden(1)
            heads(1)
            gate_out(1)
            pe.wait_ge(s_gw, 1)
            for g in range(4):
                if g == 0:
                    pe.wait_ge(s_silu, NT)
                if g >= 2:
                    pe.wait_ge(s_gwT, g - 1)
                for j in range(4):
                    last = M.transpose(ps[6 + g % 2][0:E0, j * P:(j + 1) * P], gw[:, g * 4 + j, :], ident[:, :])
                last.then_inc(s_gwT_ps, 1)
            pe.wait_ge(s_bhA, bh_evacuated(2 * NBH)[0])
            pe.wait_ge(s_bhV, bh_evacuated(2 * NBH)[1])
            pe.wait_ge(s_g, 4)
            pe.wait_ge(s_gwT, 4)
            pe.wait_ge(ld_moe, 64)

            def up(g, e):
                for c in range(2):
                    u = (g * E0 + e) * 2 + c
                    if u >= 2:
                        pe.wait_ge(s_relu, u - 1)
                    M.matmul(ps[c][:, :], W1[:, e, c * P:(c + 1) * P], xT(g), start=True, stop=True).then_inc(s_up, 1)

            def down(g, e):
                v = g * E0 + e
                pe.wait_ge(s_relu, 2 * v + 2)
                for j in range(4):
                    if e % 4 == 0 and v:
                        pe.wait_ge(s_yg, 16 * (v // 4 - 1) + 4 * j + 4)
                    for c in range(2):
                        last = M.matmul(ps[4 + j][:, (e % 4) * D:(e % 4 + 1) * D], hS[:, v % 2, c, j * P:(j + 1) * P],
                                        W2[:, 2 * e + c, :], start=(c == 0), stop=(c == 1))
                last.then_inc(s_down, 1)

            order = [(g, e) for g in range(4) for e in range(E0)]
            up(*order[0])
            for i, ge in enumerate(order):
                if i + 1 < len(order):
                    up(*order[i + 1])
                down(*ge)
            for g in range(4):
                f, j0 = g // 2, (g % 2) * 4
                pe.wait_ge(s_O, f + 1)
                pe.wait_ge(s_relu, 2 * E0 * 4)
                for j in range(4):
                    src = O[:, f * P:(f + 1) * P, j0 + j]
                    last = M.transpose(ps[g][:, j * P:(j + 1) * P], src, ident[:, :])
                last.then_inc(s_O_ps, 1)
            for g in range(4):
                pe.wait_ge(s_Og, g // 2 + 1)
                pe.wait_ge(s_yg, 128)
                for j in range(4):
                    last = M.transpose(ps[4 + g][:, j * P:(j + 1) * P], Ot[:, g * 4 + j, :], ident[:, :])
                last.then_inc(s_OT_ps, 1)
            pe.wait_ge(s_wo, 1)
            pe.wait_ge(s_Ot, 4)
            for g in range(4):
                pe.wait_ge(s_OT, g + 1)
                for j in range(4):
                    m = g * 4 + j
                    M.matmul(ps[g][:, j * D:(j + 1) * D], OT[:, m, :], wo[:, :], start=True, stop=False)
                    last = M.matmul(ps[g][:, j * D:(j + 1) * D], gwT[:, m, :], b2[:, :], start=False, stop=True)
                last.then_inc(s_out_ps, 1)


LDW = 11
CONSTS = 4 + E0 + 5


H1 = 16
PAIRS = H1 // 2
SLOT = 64
QK_ROWS = 48
ALL_ROWS = 51
ATT = 3
STEPS = ATT * B
UNIT_B = 2
UNITS = STEPS // UNIT_B
LAG = 2 * PAIRS
SLOTS = ((0, 1, 2, 0, 1, 0), (0, 0, 0, 1, 1, 2))
SCALE = float(DK) ** -0.5
PARTS = 6
WV = (8, 16, 16)
ONES_BF16X2 = float(np.array([0x3F803F80], np.uint32).view(np.float32)[0])


def scratch(nc):
    return nc.dram_tensor("qk_parts", (2 * ATT, H1, len(SLOTS[0]), DK, B * T), BF16, kind="Internal").ap()


def attention(nc, a, x1, xn1, ym, yd):
    parts_dram = scratch(nc)
    with ExitStack() as ctx:
        def sb(name, shape, dt=F32):
            return ctx.enter_context(nc.sbuf_tensor(name, shape, dt))

        def sem(name):
            return ctx.enter_context(nc.semaphore(name))

        bank = [ctx.enter_context(nc.psum_tensor(f"l1_bank{i}", [P, 512], F32)) for i in range(4)]
        wide = [ctx.enter_context(nc.psum_tensor(f"l1_wide{i}", [P, 1024], F32)) for i in range(2)]
        av_bank, tr_bank = bank[2], bank[3]
        eight = bank + [w[:, k * 512:(k + 1) * 512] for w in wide for k in range(2)]

        xT = sb("xT", [P, B, T])
        xm = ym[:, :, :].rearrange("p (b f) t -> p b (f t)", f=HALVES)
        ident = sb("ident1", [P, P])
        identb = sb("identb", [P, P], BF16)
        stat = sb("stat1", [P, 8, NT])
        bn = sb("bn", [P, 8])
        vec = sb("vec", [P, 4])
        lamv = sb("lamv", [P, 4, DK])
        lam = sb("lam", [P, 4])
        wq = sb("wq", [P, 4, D])
        wv = sb("wv", [P, 2 * D])
        wm = sb("wm", [P, 3 * D])
        part = [sb(f"part{i}", [P, 3, 512], BF16) for i in range(PARTS)]
        rest = [sb(f"rest{i}", [P, 512]) for i in range(2)]
        Q = [sb(f"Q{i}", [P, PAIRS, UNIT_B * T], BF16) for i in range(RING)]
        K = [sb(f"K{i}", [P, PAIRS, 2, UNIT_B * T], BF16) for i in range(RING)]
        vlen = [H1 * (w + 1) + 31 - w for w in (8, 16)]
        va = [sb(f"va{i}", [P, NT, vlen[i]]) for i in range(2)]
        E = sb("E", [P, 4, 2, 2, T])
        Yt = sb("Yt", [P, 2, 2, T])
        zo = sb("zo", [3, 2, UNIT_B * T], BF16)
        nm = sb("nm", [P, 2, 2, 2, PAIRS])
        nres = sb("nres", [P, 2, 2, PAIRS])
        ns = sb("ns", [P, 2, 2, 2, 3, PAIRS], BF16)
        shT = sb("shT", [48, 2, T], BF16)
        rz = sb("rz", [P, 2, 8])
        y2 = sb("y2", [P, 2, 2, 8, 16])
        Eflat = E[:, :, :, :, :].rearrange("p a b c t -> p (a b c t)")
        u0 = Eflat[:, 0:NT * D].rearrange("p (m d) -> p m d", m=NT)
        sq = Eflat[:, NT * D:2 * NT * D].rearrange("p (m d) -> p m d", m=NT)

        ld_v, ld_wm, ld_wa = sem("ld_v"), sem("ld_wm"), sem("ld_wa")
        s_const = sem("s_const1")
        s_cen, s_sqr, s_var, s_std, s_xn = (sem(n + "1") for n in ("s_cen", "s_sqr", "s_var", "s_std", "s_xn"))
        s_t_ps, s_xT, s_xm = sem("s_t_ps"), sem("s_xT"), sem("s_xm")
        s_bmean, s_bssq, s_bvar, s_bstd, s_bn = (sem(n) for n in ("s_bmean", "s_bssq", "s_bvar", "s_bstd", "s_bn"))
        s_u, s_lamp, s_lame = sem("s_u"), sem("s_lamp"), sem("s_lame")
        s_ch, s_hi, s_rest, s_mid, s_lo = sem("s_ch"), sem("s_hi"), sem("s_rest"), sem("s_mid"), sem("s_lo")
        s_pout = [sem(f"s_pout{i}") for i in range(PARTS // 2)]
        s_v_ps, s_v = sem("s_v_ps"), sem("s_v")
        s_kones = sem("s_kones")
        s_stack = [sem(f"s_stack{i}") for i in range(RING)]
        s_max_ps, s_max, s_split, s_sh_ps, s_shT = (sem(n) for n in ("s_max_ps", "s_max", "s_split", "s_sh_ps", "s_shT"))
        s_shift = [sem(f"s_shift{i}") for i in range(2)]
        s_T, s_E, s_AV, s_Yt, s_TR, s_norm, s_yd = (sem(n) for n in ("s_T", "s_E", "s_AV", "s_Yt", "s_TR", "s_norm", "s_yd"))
        s_dve, s_pool = sem("s_dve1"), sem("s_pool1")

        block = ctx.enter_context(nc.Block())
        CH = [(2 * at + t, 2 * quad + c) for at in range(ATT) for quad in range(2) for c in range(2) for t in range(2)]
        CONST1 = 6 + 2 * RING
        NW = 2 * STEPS
        FIRST_CH = 8

        def chunk_of(gp):
            i = FIRST_CH + gp // PAIRS
            return i if gp % PAIRS == PAIRS - 1 and gp >= 0 and i < len(CH) else 0

        def chunk_bank(i):
            return (eight[i % 4] if i < FIRST_CH else tr_bank)[:, :]

        GP = range(-LAG, STEPS * PAIRS + 4)

        @block.sync
        def _(sp):
            for n, name in enumerate(("bn_gamma", "bn_beta")):
                sp.dma_start(vec[:, n:n + 1], a[f"L1_attn_{name}"].unsqueeze(1)).then_inc(ld_v, 16)
            for n, name in enumerate(("ln1_w", "ln1_b")):
                sp.dma_start(vec[:, 2 + n:3 + n], a[f"L1_ffn_{name}"].unsqueeze(1)).then_inc(ld_v, 16)
            for n, name in enumerate(("lq1", "lk1", "lq2", "lk2")):
                sp.dma_start(lamv[:, n, :], a[f"L1_attn_{name}"].partition_broadcast(P)).then_inc(ld_v, 16)
            sp.dma_start(wm[:, :], a["L1_ffn_w_qkv"]).then_inc(ld_wm, 16)
            for n, name in enumerate(("q1", "k1", "q2", "k2")):
                sp.dma_start(wq[:, n, :], a[f"L1_attn_{name}_wT"]).then_inc(ld_wa, 16)
            sp.dma_start(wv[:, :], a["L1_attn_v_wT"]).then_inc(ld_wa, 16)

            def store(i):
                ten, c = CH[i]
                sp.wait_ge(s_lo, i + 1)
                for slot, pn in enumerate(SLOTS[ten % 2]):
                    sp.dma_start(parts_dram[ten, :, slot, :, c * 512:(c + 1) * 512], part[i % PARTS][:, pn, :])\
                        .then_inc(s_pout[i // 2 % (PARTS // 2)], 16)

            def load(v):
                if v >= RING:
                    sp.wait_ge(s_T, PAIRS * UNIT_B * (v - RING + 1))
                sp.wait_ge(s_pout[v % (PARTS // 2)], 192 * (v // (PARTS // 2) + 1))
                at, quad = v // (B // UNIT_B), v % (B // UNIT_B)
                cols = slice(quad * UNIT_B * T, (quad + 1) * UNIT_B * T)
                for hp in range(2):
                    for which in range(2):
                        dst = Q[v % RING] if which == 0 else K[v % RING][:, :, hp, :]
                        src = parts_dram[2 * at + which, :, :, :, cols].rearrange("(p h) n d t -> h (n d) p t", h=2)
                        sp.dma_start(dst[SLOT * hp:SLOT * hp + QK_ROWS], src[hp]).then_inc(s_stack[v % RING], 16)
                    sp.dma_start(Q[v % RING][SLOT * hp + QK_ROWS:SLOT * hp + ALL_ROWS, :, :], zo[:, 0:1, :].to_broadcast([3, PAIRS, UNIT_B * T]))\
                        .then_inc(s_stack[v % RING], 16)

            def shift(st):
                sp.wait_ge(s_shT, st + 1)
                v, b = st // UNIT_B, st % UNIT_B
                for hp in range(2):
                    row = SLOT * hp + QK_ROWS
                    sp.dma_start(Q[v % RING][row:row + 3, :, b * T:(b + 1) * T],
                                 shT[24 * hp:24 * hp + 24, st % 2, :]).then_inc(s_shift[st % 2], 16)

            sp.wait_ge(s_const, CONST1)
            for i in range(RING):
                for hp in range(2):
                    sp.dma_start(K[i][SLOT * hp + QK_ROWS:SLOT * hp + ALL_ROWS, :, hp, :],
                                 zo[:, 1:2, :].to_broadcast([3, PAIRS, UNIT_B * T])).then_inc(s_kones, 16)
            for v in range(FIRST_CH // 2):
                store(2 * v)
                store(2 * v + 1)
                if 1 <= v <= RING:
                    load(v - 1)
            for st in range(STEPS):
                if st >= 2 and FIRST_CH + st - 2 < len(CH):
                    store(FIRST_CH + st - 2)
                shift(st)
                if st % UNIT_B == 0 and st // UNIT_B + 2 in range(RING, UNITS):
                    load(st // UNIT_B + 2)

        @block.gpsimd
        def _(pool):
            V = nc.gpsimd
            n = 0

            def chain(ins):
                nonlocal n
                ins.then_inc(s_pool, 1)
                n += 1
                pool.wait_ge(s_pool, n)

            chain(V.memset(ident[:, :], 0.0))
            V.affine_select(out=ident[:, :], in_=ident[:, :], compare_op=ALU.not_equal, fill=1.0, base=0,
                            pattern=[[-1, P]], channel_multiplier=1).then_inc(s_const, 1)
            pool.wait_ge(s_const, 1)
            V.tensor_copy(identb[:, :], ident[:, :]).then_inc(s_const, 1)
            for i in range(2):
                V.memset(va[i][:, :, :], 1.0).then_inc(s_const, 1)
            for i in range(RING):
                V.memset(K[i][:, :, :, :].rearrange("p a h t -> p (a h t)").bitcast(F32), 0.0).then_inc(s_const, 1)
                V.memset(Q[i][:, :, :].rearrange("p a t -> p (a t)").bitcast(F32), 0.0).then_inc(s_const, 1)
            V.memset(zo[:, 0, :], 0.0).then_inc(s_const, 1)
            V.memset(zo[:, 1, :], 1.0).then_inc(s_const, 1)

            def low(i):
                pool.wait_ge(s_mid, i + 1)
                V.tensor_tensor(part[i % PARTS][:, 2, :], rest[i % 2][:, :], part[i % PARTS][:, 1, :], ALU.subtract).then_inc(s_lo, 1)

            for i in range(FIRST_CH):
                low(i)
            for gp in GP:
                if gp % PAIRS == 0 and chunk_of(gp - 1):
                    low(chunk_of(gp - 1))
                mp = gp + LAG
                if mp % PAIRS == PAIRS - 1 and mp < STEPS * PAIRS:
                    st = mp // PAIRS
                    pool.wait_ge(s_max, H1 * (st + 1))
                    if st >= 2:
                        pool.wait_ge(s_sh_ps, st - 1)
                    src, dst = nm[:, st % 2], ns[:, st % 2]
                    for f in range(2):
                        chain(V.tensor_copy(dst[:, f, :, 0, :], src[:, f]))
                        chain(V.tensor_tensor(nres[:, f], src[:, f], dst[:, f, :, 0, :], ALU.subtract))
                        chain(V.tensor_copy(dst[:, f, :, 1, :], nres[:, f]))
                        V.tensor_tensor(dst[:, f, :, 2, :], nres[:, f], dst[:, f, :, 1, :], ALU.subtract).then_inc(s_split, 1)
                if gp % 4 == 2 and gp >= 6:
                    w = (gp - 6) // 4
                    st, hb = w // 2, (w % 2) * 8
                    at, b = st // B, st % B
                    if at == 2:
                        pool.wait_ge(s_norm, w + 1)
                        for f in range(2):
                            dst = yd[:, f * B + b, hb * 16:(hb + 8) * 16]
                            V.tensor_tensor(dst, dst, y2[:, w % 2, f].rearrange("p h e -> p (h e)"), ALU.add).then_inc(s_yd, 1)

        @block.scalar
        def _(act):
            A = nc.scalar
            for f in range(HALVES):
                act.wait_ge(s_cen, f + 1)
                A.activation(sq[:, f * B:(f + 1) * B, :], xn1[:, f * B:(f + 1) * B, :], ACT.Square).then_inc(s_sqr, 1)
            for f in range(HALVES):
                act.wait_ge(s_var, f + 1)
                A.activation(stat[:, 2, f * B:(f + 1) * B], stat[:, 1, f * B:(f + 1) * B], ACT.Sqrt).then_inc(s_std, 1)
            act.wait_ge(s_cen, 3)
            A.activation(sq[:, :, :], u0, ACT.Square).then_inc(s_sqr, 1)
            act.wait_ge(s_var, 3)
            A.activation(stat[:, 5, :], stat[:, 4, :], ACT.Sqrt).then_inc(s_std, 1)
            for g in range(4):
                f, b0 = g // 2, (g % 2) * 4
                act.wait_ge(s_t_ps, g + 1)
                A.activation(xT[:, b0:b0 + 4, f * P:(f + 1) * P], eight[g][:, :].rearrange("p (b t) -> p b t", b=4),
                             ACT.Copy).then_inc(s_xT, 1)
            act.wait_ge(ld_v, 16 * 8)
            for g in range(4):
                f, b0 = g // 2, (g % 2) * 4
                act.wait_ge(s_t_ps, g + 5)
                A.activation(xm[:, b0:b0 + 4, f * P:(f + 1) * P], eight[4 + g][:, :].rearrange("p (b t) -> p b t", b=4),
                             ACT.Identity, scale=vec[:, 2:3], bias=vec[:, 3:4]).then_inc(s_xm, 1)
            act.wait_ge(s_bmean, 1)
            act.wait_ge(s_var, 3)
            A.activation(sq[:, :, :].rearrange("p m d -> p (m d)"), xT[:, :, :].rearrange("p b t -> p (b t)"), ACT.Square,
                         bias=bn[:, 1:2], accum_out=bn[:, 2:3]).then_inc(s_bssq, 1)
            act.wait_ge(s_bvar, 1)
            A.activation(bn[:, 4:5], bn[:, 3:4], ACT.Sqrt).then_inc(s_bstd, 1)
            act.wait_ge(s_lamp, 1)
            A.activation(lam[:, 0:2], lam[:, 0:2], ACT.Exp).then_inc(s_lame, 1)

            def mid(i):
                act.wait_ge(s_rest, i + 1)
                A.activation(part[i % PARTS][:, 1, :], rest[i % 2][:, :], ACT.Copy).then_inc(s_mid, 1)

            def high(i):
                act.wait_ge(s_ch, i + 1)
                if i >= PARTS:
                    act.wait_ge(s_pout[i // 2 % (PARTS // 2)], 192 * (i // PARTS))
                A.activation(part[i % PARTS][:, 0, :], chunk_bank(i), ACT.Copy).then_inc(s_hi, 1)

            for i in range(FIRST_CH):
                high(i)
                if i:
                    mid(i - 1)
            mid(FIRST_CH - 1)
            for gp in GP:
                if 0 <= gp < STEPS * PAIRS:
                    act.wait_ge(s_T, gp + 1)
                    if gp >= 4:
                        act.wait_ge(s_AV, (gp - 4) // 2 + 1)
                    A.activation(E[:, gp % 4].rearrange("p h s t -> p (h s t)"), wide[gp % 2][:, :], ACT.Exp,
                                 scale=SCALE).then_inc(s_E, 1)
                if chunk_of(gp):
                    high(chunk_of(gp))
                if gp % PAIRS == 0 and chunk_of(gp - 1):
                    mid(chunk_of(gp - 1))
                if gp >= 4 and gp % 4 == 0:
                    w = gp // 4 - 1
                    if w < NW:
                        act.wait_ge(s_AV, 2 * w + 2)
                        if w >= 2:
                            act.wait_ge(s_TR, w - 1)
                        A.activation(Yt[:, w % 2].rearrange("p g t -> p (g t)"), av_bank[:, :], ACT.Copy).then_inc(s_Yt, 1)

        @block.vector
        def _(dve):
            V = nc.vector
            n = 0

            def link(ins):
                nonlocal n
                ins.then_inc(s_dve, 1)
                n += 1
                dve.wait_ge(s_dve, n)

            def centre(src, dst, lo, hi, row, done):
                full = [P, hi - lo, D]
                link(V.tensor_reduce(stat[:, row, lo:hi], src[:, lo:hi, :], AX_X, ALU.add))
                link(V.tensor_scalar(stat[:, row, lo:hi], stat[:, row, lo:hi], 1.0 / D, None, ALU.mult))
                V.tensor_tensor(dst[:, lo:hi, :], src[:, lo:hi, :], stat[:, row, lo:hi].unsqueeze(2).to_broadcast(full),
                                ALU.subtract).then_inc(done, 1)

            def variance(lo, hi, row):
                link(V.tensor_reduce(stat[:, row, lo:hi], sq[:, lo:hi, :], AX_X, ALU.add))
                V.tensor_scalar(stat[:, row, lo:hi], stat[:, row, lo:hi], 1.0 / D, LN_EPS, ALU.mult, ALU.add).then_inc(s_var, 1)

            def scale_by(dst, lo, hi, row, done):
                full = [P, hi - lo, D]
                link(V.reciprocal(stat[:, row, lo:hi], stat[:, row, lo:hi]))
                V.tensor_tensor(dst[:, lo:hi, :], dst[:, lo:hi, :], stat[:, row, lo:hi].unsqueeze(2).to_broadcast(full),
                                ALU.mult).then_inc(done, 1)

            for f in range(HALVES):
                centre(x1, xn1, f * B, (f + 1) * B, 0, s_cen)
            for f in range(HALVES):
                dve.wait_ge(s_sqr, f + 1)
                variance(f * B, (f + 1) * B, 1)
            for f in range(HALVES):
                dve.wait_ge(s_std, f + 1)
                scale_by(xn1, f * B, (f + 1) * B, 2, s_xn)
            dve.wait_ge(s_xn, 2)
            centre(xn1, u0, 0, NT, 3, s_cen)
            dve.wait_ge(s_sqr, 3)
            variance(0, NT, 4)
            dve.wait_ge(s_std, 3)
            scale_by(u0, 0, NT, 5, s_u)
            xf = xT[:, :, :].rearrange("p b t -> p (b t)")
            dve.wait_ge(s_xT, 4)
            link(V.tensor_reduce(bn[:, 0:1], xf, AX_X, ALU.add))
            V.tensor_scalar(bn[:, 1:2], bn[:, 0:1], -1.0 / (B * T), None, ALU.mult).then_inc(s_bmean, 1)
            dve.wait_ge(s_bssq, 1)
            V.tensor_scalar(bn[:, 3:4], bn[:, 2:3], 1.0 / (B * T), LN_EPS, ALU.mult, ALU.add).then_inc(s_bvar, 1)
            dve.wait_ge(s_bstd, 1)
            dve.wait_ge(ld_v, 16 * 8)
            dve.wait_ge(s_bmean, 1)
            link(V.reciprocal(bn[:, 5:6], bn[:, 4:5]))
            link(V.tensor_tensor(bn[:, 5:6], bn[:, 5:6], vec[:, 0:1], ALU.mult))
            link(V.tensor_scalar(xf, xf, bn[:, 1:2], bn[:, 5:6], ALU.add, ALU.mult))
            V.tensor_scalar(xf, xf, vec[:, 1:2], None, ALU.add).then_inc(s_bn, 1)
            link(V.tensor_tensor(lamv[:, 0, :], lamv[:, 0, :], lamv[:, 1, :], ALU.mult))
            link(V.tensor_tensor(lamv[:, 2, :], lamv[:, 2, :], lamv[:, 3, :], ALU.mult))
            link(V.tensor_reduce(lam[:, 0:1], lamv[:, 0, :], AX_X, ALU.add))
            V.tensor_reduce(lam[:, 1:2], lamv[:, 2, :], AX_X, ALU.add).then_inc(s_lamp, 1)
            dve.wait_ge(s_lame, 1)
            link(V.tensor_tensor(lam[:, 2:3], lam[:, 1:2], lam[:, 0:1], ALU.subtract))
            link(V.tensor_scalar(lam[:, 2:3], lam[:, 2:3], LAMBDA_INIT, None, ALU.subtract))

            def values(k):
                i, per = (0, 4) if k < 4 else (1, 2)
                t0 = k * 4 if k < 4 else (k - 4) * 2
                w = (8, 16)[i]
                dve.wait_ge(s_v_ps, k + 1)
                V.tensor_copy(va[i][:, t0:t0 + per, 0:H1 * (w + 1)].rearrange("p m (h e) -> p m h e", h=H1)[:, :, :, 0:w],
                              eight[4 + k % 4][:, :].rearrange("p (m h e) -> p m h e", m=per, h=H1)).then_inc(s_v, 1)

            dve.wait_ge(s_const, CONST1)

            def remainder(i):
                dve.wait_ge(s_hi, i + 1)
                if i >= 2:
                    dve.wait_ge(s_lo, i - 1)
                V.tensor_tensor(rest[i % 2][:, :], chunk_bank(i), part[i % PARTS][:, 0, :], ALU.subtract).then_inc(s_rest, 1)

            for i in range(FIRST_CH):
                remainder(i)
                if i % 2 == 1:
                    values(i // 2)
            for k in range(4, 12):
                values(k)

            for gp in GP:
                mp = gp + LAG
                if mp < STEPS * PAIRS:
                    st, p = mp // PAIRS, mp % PAIRS
                    if p == 0 and st >= 2:
                        dve.wait_ge(s_split, 2 * (st - 1))
                    for f in range(2):
                        dve.wait_ge(s_max_ps, 2 * mp + f + 1)
                        V.tensor_reduce(nm[:, st % 2, f, :, p], bank[f][:, :].rearrange("p (h t) -> p h t", h=2),
                                        AX_X, ALU.max, negate=True).then_inc(s_max, 1)
                if gp % PAIRS == 4 and 0 <= gp // PAIRS + 1 < STEPS:
                    st = gp // PAIRS + 1
                    dve.wait_ge(s_sh_ps, st + 1)
                    if st >= 2:
                        dve.wait_ge(s_shift[st % 2], 32 * (st // 2))
                    V.tensor_copy(shT[:, st % 2, :], tr_bank[0:48, 0:T // 2].bitcast(BF16)).then_inc(s_shT, 1)
                if gp % 4 == 2 and gp >= 6:
                    w = (gp - 6) // 4
                    st, hb = w // 2, (w % 2) * 8
                    at, b = st // B, st % B
                    wd = WV[at]
                    dve.wait_ge(s_TR, w + 1)
                    src = tr_bank[:, :].rearrange("p (f h e) -> p f h e", f=2, h=8)
                    link(V.reciprocal(rz[:, :, :], src[:, :, :, wd]))
                    if at == 2:
                        link(V.tensor_scalar(rz[:, :, :], rz[:, :, :], lam[:, 2:3], None, ALU.mult))
                        if w >= 4 * B + 2:
                            dve.wait_ge(s_yd, 2 * (w - 4 * B - 1))
                    for f in range(2):
                        if at == 0:
                            dst = ym[:, f * B + b, hb * 8:(hb + 8) * 8].rearrange("p (h e) -> p h e", e=8)
                        elif at == 1:
                            dst = yd[:, f * B + b, hb * 16:(hb + 8) * 16].rearrange("p (h e) -> p h e", e=16)
                        else:
                            dst = y2[:, w % 2, f]
                        ins = V.tensor_tensor(dst, src[:, f, :, 0:wd], rz[:, f, :].unsqueeze(2).to_broadcast([P, 8, wd]), ALU.mult)
                        if f == 0:
                            ins.then_inc(s_dve, 1)
                            n += 1
                        else:
                            ins.then_inc(s_norm, 1)
                    dve.wait_ge(s_norm, w + 1)
                if chunk_of(gp):
                    remainder(chunk_of(gp))

        @block.tensor
        def _(pe):
            M = nc.tensor
            pe.wait_ge(s_const, 2)
            for g in range(4):
                pe.wait_ge(s_xn, g // 2 + 1)
                for j in range(4):
                    last = M.transpose(eight[g][:, j * P:(j + 1) * P], xn1[:, g * 4 + j, :], ident[:, :])
                last.then_inc(s_t_ps, 1)
            pe.wait_ge(s_u, 1)
            for g in range(4):
                for j in range(4):
                    last = M.transpose(eight[4 + g][:, j * P:(j + 1) * P], u0[:, g * 4 + j, :], ident[:, :])
                last.then_inc(s_t_ps, 1)

            def project_v(k):
                i, per = (0, 4) if k < 4 else (1, 2)
                t0 = k * 4 if k < 4 else (k - 4) * 2
                if k >= 4:
                    pe.wait_ge(s_v, k - 3)
                src, w, lo = (xm, wm, 2 * D) if i == 0 else (xT, wv, 0)
                width = 512 // per
                for j in range(per):
                    m = t0 + j
                    f, b = m // B, m % B
                    last = M.matmul(eight[4 + k % 4][:, j * width:(j + 1) * width], src[:, b, f * P:(f + 1) * P],
                                    w[:, lo:lo + width], start=True, stop=True)
                last.then_inc(s_v_ps, 1)

            pe.wait_ge(s_xT, 4)
            pe.wait_ge(s_xm, 4)
            pe.wait_ge(ld_wm, 16)

            def chunk(i):
                ten, c = CH[i]
                w = wm[:, ten * D:(ten + 1) * D] if ten < 2 else wq[:, ten - 2, :]
                src = xm if ten < 2 else xT
                M.matmul(chunk_bank(i), w, src[:, 2 * c:2 * c + 2, :].rearrange("p b t -> p (b t)"),
                         start=True, stop=True).then_inc(s_ch, 1)

            for i in range(FIRST_CH):
                if i >= 4:
                    pe.wait_ge(s_rest, i - 3)
                chunk(i)
                if i % 2 == 1:
                    project_v(i // 2)
            pe.wait_ge(s_bn, 1)
            pe.wait_ge(ld_wa, 80)
            for k in range(4, 12):
                project_v(k)
            pe.wait_ge(s_rest, FIRST_CH)
            pe.wait_ge(s_v, 12)


            def maxima(mp, f):
                if mp >= STEPS * PAIRS:
                    return
                st, p = mp // PAIRS, mp % PAIRS
                v, c0 = st // UNIT_B, (st % UNIT_B) * T
                if f == 0 and p == 0 and st % UNIT_B == 0:
                    pe.wait_ge(s_stack[v % RING], 16 * STACK_DMAS * (v // RING + 1))
                    pe.wait_ge(s_kones, 32 * RING)
                if mp:
                    pe.wait_ge(s_max, 2 * mp - 1 + f)
                M.matmul(bank[f][:, :], Q[v % RING][:, p, c0 + f * P:c0 + (f + 1) * P], K[v % RING][:, p, :, c0:c0 + T],
                         start=True, stop=True).then_inc(s_max_ps, 1)

            for gp in GP:
                maxima(gp + LAG, 0)
                if gp % PAIRS == 4 and 0 <= gp // PAIRS + 1 < STEPS:
                    st = gp // PAIRS + 1
                    pe.wait_ge(s_split, 2 * (st + 1))
                    if gp >= 6:
                        pe.wait_ge(s_norm, (gp - 6) // 4 + 1)
                    for f in range(2):
                        last = M.transpose(tr_bank[0:48, 0:T // 2].bitcast(BF16)[:, f * P:(f + 1) * P],
                                           ns[:, st % 2, f].rearrange("p h r q -> p (h r q)"), identb[:, :])
                    last.then_inc(s_sh_ps, 1)
                if 0 <= gp < STEPS * PAIRS:
                    st, p = gp // PAIRS, gp % PAIRS
                    v, c0 = st // UNIT_B, (st % UNIT_B) * T
                    if p == 0:
                        pe.wait_ge(s_shift[st % 2], 32 * (st // 2 + 1))
                    if gp == 0:
                        for _ in range(WARM):
                            M.matmul(wide[0][:, 0:3 * D], ident[:, :], wm[:, :], start=True, stop=True)
                    if gp >= 2:
                        pe.wait_ge(s_E, gp - 1)
                    for hp in range(2):
                        for f in range(2):
                            last = M.matmul(wide[gp % 2][:, hp * 512 + f * T:hp * 512 + (f + 1) * T],
                                            K[v % RING][:, p, hp, c0 + f * P:c0 + (f + 1) * P],
                                            Q[v % RING][:, p, c0:c0 + T], start=True, stop=True)
                    last.then_inc(s_T, 1)
                maxima(gp + LAG, 1)
                if gp >= 2 and gp % 2 == 0 and gp <= STEPS * PAIRS:
                    qd = gp // 2 - 1
                    st = qd // 4
                    at, b = st // B, st % B
                    i, wd = min(at, 1), WV[at] + 1
                    pe.wait_ge(s_E, gp)
                    if qd % 2 == 0 and qd >= 2:
                        pe.wait_ge(s_Yt, qd // 2)
                    for f in range(2):
                        for hh in range(4):
                            h = (qd % 4) * 4 + hh
                            last = M.matmul(av_bank[32 * hh:32 * hh + 32, (qd % 2) * T:(qd % 2 + 1) * T],
                                            va[i][:, f * B + b, h * wd:h * wd + 32],
                                            E[:, (2 * qd + hh // 2) % 4, hh % 2, f, :], start=(f == 0), stop=(f == 1))
                    last.then_inc(s_AV, 1)
                if gp % 4 == 2 and gp >= 6:
                    w = (gp - 6) // 4
                    pe.wait_ge(s_Yt, w + 1)
                    if w:
                        pe.wait_ge(s_norm, w)
                    if 0 <= (gp - 2) // PAIRS + 1 and gp % PAIRS == 6:
                        pe.wait_ge(s_shT, min((gp - 2) // PAIRS + 2, STEPS))
                    if gp % PAIRS == 2 and chunk_of(gp - 3):
                        pe.wait_ge(s_rest, chunk_of(gp - 3) + 1)
                    for f in range(2):
                        for g in range(2):
                            last = M.transpose(tr_bank[:, (2 * f + g) * P:(2 * f + g + 1) * P],
                                               Yt[:, w % 2, g, f * P:(f + 1) * P], ident[:, :])
                    last.then_inc(s_TR, 1)
                if chunk_of(gp):
                    pe.wait_ge(s_norm, (gp - 7) // 4 + 1)
                    chunk(chunk_of(gp))


STACK_DMAS = 6
RING = 3
WARM = 8
LAMBDA_INIT = 0.8 - 0.6 * math.exp(-0.3)


E1, F1 = 8, 512
FC1 = F1 // P
SLOTS1 = NT + E1 - 1
XG = 4
XGROUPS = [(t, min(t + XG, SLOTS1)) for t in range(0, SLOTS1, XG)]
XLOADS = ((0, XG), (XG, 3 * XG), (3 * XG, SLOTS1))
WB, WG = 12, 3
ROW = 2 * D + 1
NOWHERE = float(1 << 20)
U32 = mybir.dt.uint32


def finish(nc, a, x1, xn1, ym, yd, out):
    sorted_x = nc.dram_tensor("sorted_x", (SLOTS1 * P, ROW), F32, kind="Internal").ap()
    out_rows = out.rearrange("b t d -> (b t) d")
    with ExitStack() as ctx:
        def sb(name, shape, dt=F32):
            return ctx.enter_context(nc.sbuf_tensor(name, shape, dt))

        def sem(name):
            return ctx.enter_context(nc.semaphore(name))

        ps = [ctx.enter_context(nc.psum_tensor(f"l2_bank{i}", [P, 512], F32)) for i in range(8)]
        ident = sb("ident2", [P, P])
        pad = sb("pad2", [P, ROW])
        tri = sb("tri2", [P, P])
        full1 = sb("full1", [P, P])
        wx = sb("wx", [P, WB, 2 * F1])
        tno = sb("tno", [P, SLOTS1])
        wp = sb("wp", [P, D])
        cwt = sb("cwt", [P, 2, D])
        subln = sb("subln", [P, 1])
        ln2 = sb("ln2", [P, 2])
        gwt = sb("gwt", [P, E1])
        gb = sb("gb", [P, E1])
        sqd = sb("sqd", [P, NT, 2 * D])
        rs = sb("rs", [P, NT * H1])
        ymT = sb("ymT", [P, NT, P])
        ydT = sb("ydT", [P, 2, NT, P])
        x2 = sb("x2", [P, NT, D])
        tok = sb("tok2", [P, NT, ROW])
        u2, total, place = tok[:, :, 0:D], tok[:, :, D:2 * D], tok[:, :, 2 * D:ROW]
        xfT = sb("xfT", [P, NT, P])
        sq = xfT
        stat = sb("stat2", [P, 3, NT])
        lg = sb("lg2", [P, NT, E1])
        oh = sb("oh", [P, NT, E1])
        gm = sb("gm2", [P, NT])
        iota8 = sb("iota82", [P, E1])
        pre = sb("pre2", [P, 2, NT // 2 + NT, E1])
        ends = sb("ends2", [P, 2, E1 // 2 + E1])
        rank = sb("rank2", [P, NT, E1])
        cmp = sb("cmp2", [P, SLOTS1, E1])
        cnt = sb("cnt2", [P, 2, E1])
        eid = sb("eid2", [P, SLOTS1])
        pos_i = sb("pos_i", [P, NT], U32)
        wrow_i = sb("wrow_i", [P, SLOTS1], U32)
        xg = sb("xg2", [P, SLOTS1, ROW])
        xgT = sqd[:, :, :].rearrange("p m (c t) -> p (m c) t", c=2)
        hS = sb("hS2", [P, 2, F1])
        yS = ydT[:, :, :, :].rearrange("p c m t -> p (c m) t")
        place_i = sb("place_i", [P, SLOTS1], U32)
        acc = x1

        ld_p, ld_c, s_zero = sem("ld_p"), sem("ld_c"), sem("s_zero")
        s_rows, s_scat = sem("s_rows"), sem("s_scat")
        s_w = [sem(f"s_w{i}") for i in range(WB // WG)]
        s_xg = [sem(f"s_xg{i}") for i in range(len(XLOADS))]
        s_const = sem("s_const2")
        s_ym_ps, s_ymT, s_x2_ps, s_x2, s_cen, s_sqr, s_var, s_std, s_u = (
            sem(n + "_2") for n in ("s_ym_ps", "s_ymT", "s_x2_ps", "s_x2", "s_cen", "s_sqr", "s_var", "s_std", "s_u"))
        s_ysq, s_yvar, s_ystd, s_y, s_yT_ps, s_yT, s_cw, s_o_ps, s_o = (
            sem(n + "_2") for n in ("s_ysq", "s_yvar", "s_ystd", "s_y", "s_yT_ps", "s_yT", "s_cw", "s_o_ps", "s_o"))
        s_f_ps, s_f, s_lg_ps, s_lg, s_oh = (sem(n + "_2") for n in ("s_f_ps", "s_f", "s_lg_ps", "s_lg", "s_oh"))
        s_up, s_gelu, s_down, s_yS, s_sum, s_out = (
            sem(n + "_2") for n in ("s_up", "s_gelu", "s_down", "s_yS", "s_sum", "s_out"))
        s_dve, s_pool = sem("s_dve2"), sem("s_pool2")
        block = ctx.enter_context(nc.Block())
        CONST2 = 7 + NT + E1 + SLOTS1

        @block.sync
        def _(sp):
            sp.dma_start(wp[:, :], a["L1_ffn_w_proj"]).then_inc(ld_p, 16)
            for n, name in enumerate(("ln2_w", "ln2_b")):
                sp.dma_start(ln2[:, n:n + 1], a[f"L1_ffn_{name}"].unsqueeze(1)).then_inc(ld_p, 16)
            sp.dma_start(gwt[:, :], a["L1_ffn_gate_w"]).then_inc(ld_p, 16)
            sp.dma_start(gb[:, :], a["L1_ffn_gate_b"].partition_broadcast(P)).then_inc(ld_p, 16)
            sp.dma_start(cwt[:, :, :], a["L1_attn_c_wT"].rearrange("(c p) d -> p c d", p=P)).then_inc(ld_c, 16)
            for i in range(H1 // 2):
                sp.dma_start(subln[16 * i:16 * i + 16, :], a["L1_attn_subln_w"].unsqueeze(1)).then_inc(ld_c, 16)
            sp.wait_ge(s_const, CONST2)
            sp.dma_start(sorted_x.rearrange("(t p) d -> p t d", p=P),
                         pad[:, :].unsqueeze(1).to_broadcast([P, SLOTS1, ROW])).then_inc(s_zero, 16)
            sp.wait_ge(s_scat, 16 * NT)
            for i, (t0, t1) in enumerate(XLOADS):
                sp.dma_start(xg[:, t0:t1, :], sorted_x.rearrange("(t p) d -> p t d", p=P)[:, t0:t1, :]).then_inc(s_xg[i], 16)

        @block.gpsimd
        def _(pool):
            V = nc.gpsimd
            n = 0

            def chain(ins):
                nonlocal n
                ins.then_inc(s_pool, 1)
                n += 1
                pool.wait_ge(s_pool, n)

            chain(V.memset(ident[:, :], 0.0))
            V.affine_select(out=ident[:, :], in_=ident[:, :], compare_op=ALU.not_equal, fill=1.0, base=0,
                            pattern=[[-1, P]], channel_multiplier=1).then_inc(s_const, 1)
            V.memset(pre[:, :, :, :], 0.0).then_inc(s_const, 1)
            V.memset(ends[:, :, :], 0.0).then_inc(s_const, 1)
            V.memset(full1[:, :], 1.0).then_inc(s_const, 1)
            V.memset(pad[:, 0:2 * D], 0.0).then_inc(s_const, 1)
            V.memset(pad[:, 2 * D:ROW], NOWHERE).then_inc(s_const, 1)
            for m in range(NT):
                V.memset(place[:, m, :], float(m % B * T + m // B * P)).then_inc(s_const, 1)
            chain(V.memset(tri[:, :], 1.0))
            V.affine_select(out=tri[:, :], in_=tri[:, :], compare_op=ALU.is_ge, fill=0.0, base=-1,
                            pattern=[[1, P]], channel_multiplier=-1).then_inc(s_const, 1)
            for t in range(SLOTS1):
                V.memset(tno[:, t:t + 1], float(t)).then_inc(s_const, 1)
            for e in range(E1):
                V.memset(iota8[:, e:e + 1], float(E1 - e)).then_inc(s_const, 1)
            pool.wait_ge(s_x2, 4)
            for g in range(4):
                V.tensor_tensor(acc[:, 4 * g:4 * g + 4, :], acc[:, 4 * g:4 * g + 4, :], x2[:, 4 * g:4 * g + 4, :],
                                ALU.add).then_inc(s_sum, 1)

            def weights(t):
                if t >= WB:
                    pool.wait_ge(s_down, t - WB + 1)
                V.indirect_dma_start(wx[:, t % WB, :], None, a["L1_ffn_w12"],
                                     bass.IndirectOffsetOnAxis(ap=wrow_i[:, t:t + 1], axis=0)).then_inc(s_w[t % WB // WG], 16)

            pool.wait_ge(s_rows, 1)
            weights(0)
            pool.wait_ge(s_rows, 2)
            pool.wait_ge(s_zero, 16)
            for m in range(NT):
                pool.wait_ge(s_o, m // 4 + 1)
                V.indirect_dma_start(sorted_x, bass.IndirectOffsetOnAxis(ap=pos_i[:, m:m + 1], axis=0),
                                     tok[:, m, :], None).then_inc(s_scat, 16)
            for t in range(1, WB):
                weights(t)
            for t in range(SLOTS1):
                pool.wait_ge(s_yS, t + 1)
                V.indirect_dma_start(out_rows, bass.IndirectOffsetOnAxis(ap=place_i[:, t:t + 1], axis=0), yS[:, t, :], None,
                                     bounds_check=B * T - 1, oob_is_err=False).then_inc(s_out, 16)
                if t + WB < SLOTS1:
                    weights(t + WB)
            pool.wait_ge(s_out, 16 * SLOTS1)

        @block.scalar
        def _(act):
            A = nc.scalar
            for g in range(4):
                act.wait_ge(s_ym_ps, g + 1)
                A.activation(ymT[:, 4 * g:4 * g + 4, :].rearrange("p m t -> p (m t)"), ps[g][:, :], ACT.Copy).then_inc(s_ymT, 1)
            A.activation(sqd[:, :, :], yd[:, :, :], ACT.Square).then_inc(s_ysq, 1)
            act.wait_ge(s_cen, 1)
            A.activation(sq[:, :, :], u2[:, :, :], ACT.Square).then_inc(s_sqr, 1)
            act.wait_ge(s_var, 1)
            A.activation(stat[:, 1, :], stat[:, 1, :], ACT.Sqrt).then_inc(s_std, 1)
            act.wait_ge(ld_p, 80)
            for g in range(4):
                act.wait_ge(s_f_ps, g + 1)
                A.activation(xfT[:, 4 * g:4 * g + 4, :].rearrange("p m t -> p (m t)"), ps[4 + g][:, :], ACT.Identity,
                             scale=ln2[:, 0:1], bias=ln2[:, 1:2]).then_inc(s_f, 1)

            act.wait_ge(s_yvar, 1)
            A.activation(rs[:, :], rs[:, :], ACT.Sqrt).then_inc(s_ystd, 1)
            for i in range(8):
                act.wait_ge(s_yT_ps, i + 1)
                A.activation(ydT[:, i // 4, 4 * (i % 4):4 * (i % 4) + 4, :].rearrange("p m t -> p (m t)"), ps[i % 4][:, :],
                             ACT.Copy).then_inc(s_yT, 1)

            def columns(i):
                t0, t1 = XGROUPS[i]
                act.wait_ge(s_f_ps, 4 + i + 1)
                A.activation(xgT[:, t0:t1, :].rearrange("p m t -> p (m t)"), ps[5 + i % 2][:, 0:(t1 - t0) * P],
                             ACT.Identity, scale=ln2[:, 0:1], bias=ln2[:, 1:2]).then_inc(s_f, 1)

            columns(0)
            for t in range(SLOTS1):
                act.wait_ge(s_up, t + 1)
                if t >= 2:
                    act.wait_ge(s_down, t - 1)
                A.activation(hS[:, t % 2, :], ps[1 + t % 2][:, :], ACT.Gelu_apprx_tanh).then_inc(s_gelu, 1)
                if t % XG == 0 and t // XG + 1 < len(XGROUPS):
                    columns(t // XG + 1)

        @block.vector
        def _(dve):
            V = nc.vector
            n = 0

            def link(ins):
                nonlocal n
                ins.then_inc(s_dve, 1)
                n += 1
                dve.wait_ge(s_dve, n)

            full = [P, NT, D]
            for g in range(4):
                dve.wait_ge(s_x2_ps, g + 1)
                sl = slice(4 * g, 4 * g + 4)
                V.tensor_tensor(x2[:, sl, :], ps[4 + g][:, :].rearrange("p (m d) -> p m d", m=4), xn1[:, sl, :],
                                ALU.add).then_inc(s_x2, 1)
            dve.wait_ge(s_x2, 4)
            link(V.tensor_reduce(stat[:, 0, :], x2[:, :, :], AX_X, ALU.add))
            link(V.tensor_scalar(stat[:, 0, :], stat[:, 0, :], 1.0 / D, None, ALU.mult))
            V.tensor_tensor(u2[:, :, :], x2[:, :, :], stat[:, 0, :].unsqueeze(2).to_broadcast(full), ALU.subtract).then_inc(s_cen, 1)
            dve.wait_ge(s_sqr, 1)
            link(V.tensor_reduce(stat[:, 1, :], sq[:, :, :], AX_X, ALU.add))
            V.tensor_scalar(stat[:, 1, :], stat[:, 1, :], 1.0 / D, LN_EPS, ALU.mult, ALU.add).then_inc(s_var, 1)
            dve.wait_ge(s_std, 1)
            link(V.reciprocal(stat[:, 2, :], stat[:, 1, :]))
            V.tensor_tensor(u2[:, :, :], u2[:, :, :], stat[:, 2, :].unsqueeze(2).to_broadcast(full), ALU.mult).then_inc(s_u, 1)
            dve.wait_ge(s_ysq, 1)
            link(V.tensor_reduce(rs[:, :], sqd[:, :, :].rearrange("p m (h e) -> p (m h) e", e=16), AX_X, ALU.add))
            V.tensor_scalar(rs[:, :], rs[:, :], 1.0 / 16, 1e-5, ALU.mult, ALU.add).then_inc(s_yvar, 1)
            dve.wait_ge(s_ystd, 1)
            link(V.reciprocal(rs[:, :], rs[:, :]))
            y3 = yd[:, :, :].rearrange("p m (h e) -> p (m h) e", e=16)
            V.tensor_tensor(y3, y3, rs[:, :].unsqueeze(2).to_broadcast([P, NT * H1, 16]), ALU.mult).then_inc(s_y, 1)
            dve.wait_ge(ld_c, 16 * 9)
            V.tensor_scalar(cwt[:, :, :], cwt[:, :, :], subln[:, 0:1], 1.0 - LAMBDA_INIT, ALU.mult, ALU.mult).then_inc(s_cw, 1)
            dve.wait_ge(s_lg_ps, 1)
            dve.wait_ge(s_const, CONST2)
            fe = [P, NT, E1]
            dve.wait_ge(ld_p, 80)
            link(V.tensor_tensor(lg[:, :, :], ps[4][:, 0:NT * E1].rearrange("p (m e) -> p m e", m=NT),
                                 gb[:, :].unsqueeze(1).to_broadcast(fe), ALU.add))
            link(V.tensor_reduce(gm[:, :], lg[:, :, :], AX_X, ALU.max))
            link(V.tensor_tensor(lg[:, :, :], lg[:, :, :], gm[:, :].unsqueeze(2).to_broadcast(fe), ALU.is_equal))
            link(V.tensor_tensor(lg[:, :, :], lg[:, :, :], iota8[:, :].unsqueeze(1).to_broadcast(fe), ALU.mult))
            link(V.tensor_reduce(gm[:, :], lg[:, :, :], AX_X, ALU.max))
            V.tensor_tensor(oh[:, :, :], lg[:, :, :], gm[:, :].unsqueeze(2).to_broadcast(fe), ALU.is_equal).then_inc(s_oh, 1)
            dve.wait_ge(s_oh, 1)
            dve.wait_ge(s_lg_ps, 2)
            lo = NT // 2
            link(V.tensor_copy(pre[:, 0, lo:, :], ps[5][:, P:2 * P].rearrange("p (m e) -> p m e", m=NT)))
            for r in range(4):
                step, src, dst = 1 << r, r % 2, (r + 1) % 2
                link(V.tensor_tensor(pre[:, dst, lo:, :], pre[:, src, lo:, :], pre[:, src, lo - step:lo + NT - step, :], ALU.add))
            link(V.tensor_scalar(cnt[:, 0, :], pre[:, 0, lo + NT - 1, :], 1.0 / P, None, ALU.mult))
            fc = [P, NT, E1]
            link(V.tensor_tensor(cmp[:, 0:NT, :], cnt[:, 0, :].unsqueeze(1).to_broadcast(fc),
                                 tno[:, 0:NT].unsqueeze(2).to_broadcast(fc), ALU.is_gt))
            le = E1 // 2
            link(V.tensor_reduce(ends[:, 0, le:], cmp[:, 0:NT, :].rearrange("p t e -> p e t"), AX_X, ALU.add))
            for r in range(3):
                step, src, dst = 1 << r, r % 2, (r + 1) % 2
                link(V.tensor_tensor(ends[:, dst, le:], ends[:, src, le:], ends[:, src, le - step:le + E1 - step], ALU.add))
            fs = [P, SLOTS1, E1]
            link(V.tensor_tensor(cmp[:, :, :], tno[:, :].unsqueeze(2).to_broadcast(fs),
                                 ends[:, 1, le:].unsqueeze(1).to_broadcast(fs), ALU.is_ge))
            link(V.tensor_reduce(eid[:, :], cmp[:, :, :], AX_X, ALU.add))
            link(V.tensor_scalar(eid[:, :], eid[:, :], float(E1 - 1), float(P), ALU.min, ALU.mult))
            own = ps[5][:, 2 * P:2 * P + 1]
            link(V.tensor_tensor(eid[:, :], eid[:, :], own.to_broadcast([P, SLOTS1]), ALU.add))
            V.tensor_copy(wrow_i[:, :], eid[:, :]).then_inc(s_rows, 1)
            link(V.tensor_scalar(cnt[:, 1, :], ends[:, 1, le - 1:le + E1 - 1], float(P), None, ALU.mult))
            link(V.tensor_tensor(rank[:, :, :], ps[5][:, 0:P].rearrange("p (m e) -> p m e", m=NT),
                                 pre[:, 0, lo - 1:lo + NT - 1, :], ALU.add))
            link(V.tensor_tensor(rank[:, :, :], rank[:, :, :], cnt[:, 1, :].unsqueeze(1).to_broadcast(fe), ALU.add))
            link(V.tensor_tensor(rank[:, :, :], rank[:, :, :], oh[:, :, :], ALU.mult))
            link(V.tensor_reduce(gm[:, :], rank[:, :, :], AX_X, ALU.add))
            link(V.tensor_tensor(place[:, :, :], place[:, :, :], own.unsqueeze(1).to_broadcast([P, NT, 1]), ALU.add))
            V.tensor_copy(pos_i[:, :], gm[:, :]).then_inc(s_rows, 1)
            dve.wait_ge(s_sum, 4)
            for g in range(4):
                dve.wait_ge(s_o_ps, g + 1)
                sl = slice(4 * g, 4 * g + 4)
                V.tensor_tensor(total[:, sl, :], ps[g][:, :].rearrange("p (m d) -> p m d", m=4), acc[:, sl, :],
                                ALU.add).then_inc(s_o, 1)
            for t in range(SLOTS1):
                for i, (t0, t1) in enumerate(XLOADS):
                    if t == t0:
                        dve.wait_ge(s_xg[i], 16)
                        link(V.tensor_copy(place_i[:, t0:t1], xg[:, t0:t1, 2 * D:ROW].rearrange("p t o -> p (t o)")))
                dve.wait_ge(s_down, t + 1)
                V.tensor_tensor(yS[:, t, :], ps[3 + t % 2][:, 0:D], xg[:, t, D:2 * D], ALU.add).then_inc(s_yS, 1)

        @block.tensor
        def _(pe):
            M = nc.tensor
            pe.wait_ge(s_const, 1)
            for g in range(4):
                for j in range(4):
                    last = M.transpose(ps[g][:, j * P:(j + 1) * P], ym[:, 4 * g + j, :], ident[:, :])
                last.then_inc(s_ym_ps, 1)
            pe.wait_ge(ld_p, 80)
            for g in range(4):
                pe.wait_ge(s_ymT, g + 1)
                for j in range(4):
                    last = M.matmul(ps[4 + g][:, j * P:(j + 1) * P], ymT[:, 4 * g + j, :], wp[:, :], start=True, stop=True)
                last.then_inc(s_x2_ps, 1)
            pe.wait_ge(s_x2, 4)
            pe.wait_ge(s_u, 1)
            for g in range(4):
                for j in range(4):
                    last = M.transpose(ps[4 + g][:, j * P:(j + 1) * P], u2[:, 4 * g + j, :], ident[:, :])
                last.then_inc(s_f_ps, 1)
            pe.wait_ge(s_f, 4)
            for m in range(NT):
                last = M.matmul(ps[4][:, m * E1:(m + 1) * E1], xfT[:, m, :], gwt[:, :], start=True, stop=True)
            last.then_inc(s_lg_ps, 1)
            pe.wait_ge(s_ymT, 4)
            pe.wait_ge(s_y, 1)
            for i in range(8):
                c, g = i // 4, i % 4
                if i == 4:
                    pe.wait_ge(s_oh, 1)
                    pe.wait_ge(s_const, CONST2)
                    flat = oh[:, :, :].rearrange("p m e -> p (m e)")
                    M.matmul(ps[5][:, 0:P], tri[:, :], flat, start=True, stop=True)
                    M.matmul(ps[5][:, P:2 * P], full1[:, :], flat, start=True, stop=True)
                    M.matmul(ps[5][:, 2 * P:2 * P + 1], tri[:, :], full1[:, 0:1], start=True, stop=True).then_inc(s_lg_ps, 1)
                if i >= 4:
                    pe.wait_ge(s_yT, i - 3)
                for j in range(4):
                    last = M.transpose(ps[g][:, j * P:(j + 1) * P], yd[:, 4 * g + j, c * P:(c + 1) * P], ident[:, :])
                last.then_inc(s_yT_ps, 1)
            pe.wait_ge(s_cw, 1)
            pe.wait_ge(s_yT, 8)
            for g in range(4):
                for j in range(4):
                    for c in range(2):
                        last = M.matmul(ps[g][:, j * P:(j + 1) * P], ydT[:, c, 4 * g + j, :], cwt[:, c, :],
                                        start=(c == 0), stop=(c == 1))
                last.then_inc(s_o_ps, 1)

            def turn(i):
                t0, t1 = XGROUPS[i]
                pe.wait_ge(s_xg[min((i + 1) // 2, 2)], 16)
                if i >= 2:
                    pe.wait_ge(s_f, 4 + i - 1)
                for t in range(t0, t1):
                    last = M.transpose(ps[5 + i % 2][:, (t - t0) * P:(t - t0 + 1) * P], xg[:, t, 0:D], ident[:, :])
                last.then_inc(s_f_ps, 1)

            def up(t):
                pe.wait_ge(s_w[t % WB // WG], 16 * (t // WB * WG + min(WG, SLOTS1 - t // WG * WG)))
                pe.wait_ge(s_f, 4 + t // XG + 1)
                if t >= 2:
                    pe.wait_ge(s_gelu, t - 1)
                for c in range(FC1):
                    last = M.matmul(ps[1 + t % 2][:, c * P:(c + 1) * P], wx[:, t % WB, c * P:(c + 1) * P], xgT[:, t, :],
                                    start=True, stop=True)
                last.then_inc(s_up, 1)

            def down(t):
                pe.wait_ge(s_gelu, t + 1)
                if t >= 2:
                    pe.wait_ge(s_yS, t - 1)
                for c in range(FC1):
                    last = M.matmul(ps[3 + t % 2][:, 0:D], hS[:, t % 2, c * P:(c + 1) * P],
                                    wx[:, t % WB, F1 + c * D:F1 + (c + 1) * D], start=(c == 0), stop=(c == FC1 - 1))
                last.then_inc(s_down, 1)

            pe.wait_ge(s_rows, 2)
            pe.wait_ge(s_o, 4)
            turn(0)
            turn(1)
            up(0)
            for t in range(SLOTS1):
                if t % XG == 2 and t // XG + 2 < len(XGROUPS):
                    turn(t // XG + 2)
                if t + 1 < SLOTS1:
                    up(t + 1)
                down(t)


def build(nc, a, out):
    with ExitStack() as ctx:
        x1 = ctx.enter_context(nc.sbuf_tensor("x1", [P, NT, D], F32))
        layer0(nc, a, x1)
        xn1 = ctx.enter_context(nc.sbuf_tensor("xn1", [P, NT, D], F32))
        ym = ctx.enter_context(nc.sbuf_tensor("ym", [P, NT, D], F32))
        yd = ctx.enter_context(nc.sbuf_tensor("yd", [P, NT, 2 * D], F32))
        attention(nc, a, x1, xn1, ym, yd)
        finish(nc, a, x1, xn1, ym, yd, out)




def kernel(**inputs):
    import numpy as _np
    import concourse.bacc as _bacc
    from concourse import mybir as _mybir
    from concourse.bass_utils import run_bass_kernel_spmd as _run

    nc = _bacc.Bacc("TRN2", target_bir_lowering=False, num_devices=1)
    arrays, a = {}, {}
    laid = {k: _np.asarray(v) for k, v in inputs.items()}
    laid["L0_ffn_b1T"] = laid.pop("L0_ffn_b1").reshape(-1, P).T
    for name in ("q1_w", "q2_w", "k1_w", "k2_w", "v_w", "c_w"):
        laid[f"L1_attn_{name}T"] = laid.pop(f"L1_attn_{name}").T
    w1, w2 = laid.pop("L1_ffn_w1"), laid.pop("L1_ffn_w2")
    w2 = w2.reshape(E1, FC1, P, D).transpose(0, 2, 1, 3).reshape(E1, P, FC1 * D)
    laid["L1_ffn_w12"] = _np.concatenate([w1, w2], axis=2).reshape(E1 * P, 2 * F1)
    for name, v in laid.items():
        v = _np.ascontiguousarray(v)
        arrays[f"in_{name}"] = v
        a[name] = nc.dram_tensor(f"in_{name}", v.shape, _mybir.dt.from_np(v.dtype), kind="ExternalInput").ap()
    out = nc.dram_tensor("out_0_dram", (B, T, D), _mybir.dt.float32, kind="ExternalOutput").ap()
    build(nc, a, out)
    r = _run(nc, [arrays], core_ids=[0])
    return r.results[0]["out_0_dram"]
```
